# Optimizing a Trainium2 kernel written in Bass

```python
import numpy as np
import jax
import jax.numpy as jnp

def _softmax(x, axis=-1):
    return jax.nn.softmax(x, axis=axis)

def _gelu(x):
    return jax.nn.gelu(x, approximate=True)

def _silu(x):
    return jax.nn.silu(x)

def _sigmoid(x):
    return jax.nn.sigmoid(x)

def _layernorm(x, axis=-1, eps=1e-05):
    m = jnp.mean(x, axis=axis, keepdims=True)
    v = jnp.var(x, axis=axis, keepdims=True)
    return (x - m) / jnp.sqrt(v + eps)

def _scatter_add(tgt, idx, src, axis=0):
    return tgt.at[idx].add(src)

def _segment_sum(src, seg, n):
    return jax.ops.segment_sum(src, seg, n)
kernel_name = 'mk_adj_resnorm_d1_adj_r2_345b56'

def setup_inputs(seed: int=0):
    np.random.seed(seed)
    _w = jnp.asarray

    def _rec_inputs():
        import jax
        import jax.numpy as jnp
        _gk = jax.random.key(seed)
        x = -0.003407 + 1.001 * jax.random.normal(jax.random.fold_in(_gk, 1), (512, 128), jnp.float32)
        _a = jax.random.bernoulli(jax.random.fold_in(_gk, 2), 0.0078125, (512, 512))
        adj = _a.astype(jnp.int32)
        return (x, adj)
    x, adj = _rec_inputs()

    def _L0_gnn_setup():
        import jax, jax.numpy as jnp
        import numpy as np
        N = 512
        H = 128
        key = jax.random.key(seed)
        k1, k2, k3, k4, k5, k6, k7 = jax.random.split(key, 7)
        s = 1.0 / np.sqrt(H)
        node_features = jax.random.normal(k1, (N, H), dtype=jnp.float32)
        adjacency_matrix = jax.random.randint(k2, (N, N), 0, 2, dtype=jnp.int32)
        edge_table = jax.random.normal(k3, (N * N, H), dtype=jnp.float32)
        w_ih = jax.random.uniform(k4, (3 * H, H), minval=-s, maxval=s, dtype=jnp.float32)
        w_hh = jax.random.uniform(k5, (3 * H, H), minval=-s, maxval=s, dtype=jnp.float32)
        b_ih = jax.random.uniform(k6, (3 * H,), minval=-s, maxval=s, dtype=jnp.float32)
        b_hh = jax.random.uniform(k7, (3 * H,), minval=-s, maxval=s, dtype=jnp.float32)
        return {'node_features': node_features, 'adjacency_matrix': adjacency_matrix, 'edge_table': edge_table, 'w_ih': w_ih, 'w_hh': w_hh, 'b_ih': b_ih, 'b_hh': b_hh}
    _L0_gnn_all = _L0_gnn_setup()
    _L0_gnn_in = {k: v for k, v in _L0_gnn_all.items() if k in ('edge_table', 'w_ih', 'w_hh', 'b_ih', 'b_hh')}
    del _L0_gnn_all
    return {'x': x, 'adj': adj, 'L0_gnn_edge_table': _L0_gnn_in['edge_table'], 'L0_gnn_w_ih': _L0_gnn_in['w_ih'], 'L0_gnn_w_hh': _L0_gnn_in['w_hh'], 'L0_gnn_b_ih': _L0_gnn_in['b_ih'], 'L0_gnn_b_hh': _L0_gnn_in['b_hh']}

def reference(x, adj, L0_gnn_edge_table, L0_gnn_w_ih, L0_gnn_w_hh, L0_gnn_b_ih, L0_gnn_b_hh):
    import jax
    import jax.numpy as jnp

    def _L0_gnn_ref(node_features, adjacency_matrix, edge_table, w_ih, w_hh, b_ih, b_hh):
        import jax, jax.numpy as jnp
        import numpy as np
        N = 512
        H = 128
        n, h = node_features.shape
        T = edge_table.reshape(n, n, h)
        adj = adjacency_matrix.astype(node_features.dtype)
        agg = jnp.einsum('ij,jh,ijh->ih', adj, node_features, T)
        gi = agg @ w_ih.T + b_ih
        gh = node_features @ w_hh.T + b_hh
        ir, iz, in_ = jnp.split(gi, 3, axis=-1)
        hr, hz, hn = jnp.split(gh, 3, axis=-1)
        r = jax.nn.sigmoid(ir + hr)
        z = jax.nn.sigmoid(iz + hz)
        nn_ = jnp.tanh(in_ + r * hn)
        return (1.0 - z) * nn_ + z * node_features
    x = _layernorm(x + _L0_gnn_ref(x, adj, L0_gnn_edge_table, L0_gnn_w_ih, L0_gnn_w_hh, L0_gnn_b_ih, L0_gnn_b_hh), axis=-1)
    return x

_drawn_inputs = setup_inputs


def setup_inputs(seed=0):
    import zlib

    import numpy as np

    out = dict(_drawn_inputs(seed))
    spreads = {}
    factors = {'L0_gnn_b_ih': 3.521, 'L0_gnn_b_hh': 5.343}
    for name, (base, spread) in spreads.items():
        noise = np.random.default_rng([zlib.crc32(name.encode()), seed]).standard_normal(out[name].shape)
        drawn = base * np.exp(spread * noise) if base else spread * noise
        out[name] = jnp.asarray(drawn.astype(out[name].dtype))
    for name, factor in factors.items():
        out[name] = (out[name] * factor).astype(out[name].dtype)
    return out
```

```python
from contextlib import ExitStack

import concourse.bass as bass
from concourse import mybir

F32 = mybir.dt.float32
I32 = mybir.dt.int32
ALU = mybir.AluOpType
ACT = mybir.ActivationFunctionType
AX = mybir.AxisListType

P = 128
SLOTS = 16
DIRECT = 3
REST = SLOTS - DIRECT
WINDOWS = ((0, 2), (0, 4), (1, 5), (3, 7))
CHUNKS = WINDOWS[-1][1]
CHUNKS_PER_BANK = 3
BANK = 512
ROWS_PER_LOAD = 4
BUFFERS = 2
EPS = 1e-5


def gnn_gru_norm(nc, x, x_t, adj_t, edge_table, w_ih_t, w_hh_t, b_ih, b_hh, out):
    N, H = x.shape
    NT = N // P
    G3 = 3 * H
    INVALID = N * N
    GATHERS = NT * DIRECT + CHUNKS
    XR = H + REST + 2
    COL_LIST, COL_BASE, COL_J = H, H + REST, H + REST + 1
    STRIDE = BANK // CHUNKS_PER_BANK
    BANKS = -(-CHUNKS // CHUNKS_PER_BANK)
    groups = [range(b * CHUNKS_PER_BANK, min((b + 1) * CHUNKS_PER_BANK, CHUNKS)) for b in range(BANKS)]
    ONES_SUM = P * NT
    LOADS = N // ROWS_PER_LOAD

    with ExitStack() as ctx:
        def sb(name, shape, dt=F32):
            return ctx.enter_context(nc.sbuf_tensor(name, shape, dt))

        def psum(name, shape):
            return ctx.enter_context(nc.psum_tensor(name, shape, F32))

        def sem(name):
            return ctx.enter_context(nc.semaphore(name))

        adj_sb = sb("adj_sb", [P, NT, N], I32)
        x_sb = sb("x_sb", [P, NT, H])
        xT_sb = sb("xT_sb", [P, N])
        wih_sb = sb("wih_sb", [P, G3])
        whh_sb = sb("whh_sb", [P, G3])
        bias2 = sb("bias2", [2, BANK])
        ones2 = sb("ones2", [2, P])
        key_of_i = sb("key_of_i", [P, N])
        rank_iota = sb("rank_iota", [P, CHUNKS * P])
        rank_of = sb("rank_of", [P, CHUNKS])
        slot_iota = sb("slot_iota", [P, REST])
        flat_of_j = sb("flat_of_j", [P, NT])
        before = sb("before", [P, P])
        ones = sb("ones", [P, P])
        low = sb("low", [P, NT])
        high = sb("high", [P, NT])
        keys = sb("keys", [P, NT, N])
        keys2 = sb("keys2", [P, NT, N])
        lists = sb("lists", [P, NT, SLOTS])
        filled = sb("filled", [P, NT, SLOTS])
        idx_direct = sb("idx_direct", [P, NT, DIRECT], I32)
        rest_n = sb("rest_n", [P, NT])
        rest_end = sb("rest_end", [P, NT])
        x_rest = sb("x_rest", [P, NT, XR])
        is_before_end = sb("is_before_end", [P, NT, 4 * P])
        rank_hot = sb("rank_hot", [P, NT, 4 * P])
        slot_of = sb("slot_of", [P, CHUNKS])
        slot_eq = sb("slot_eq", [P, CHUNKS, REST])
        slot_key = sb("slot_key", [P, CHUNKS, REST])
        rest_key = sb("rest_key", [P, CHUNKS])
        rest_row = sb("rest_row", [P, CHUNKS])
        idx_rest = sb("idx_rest", [P, CHUNKS], I32)
        edge = sb("edge", [P, GATHERS, H])
        prod = sb("prod", [P, GATHERS, H])
        target_hot = sb("target_hot", [P, GATHERS, N])
        aggT = sb("aggT", [P, N])
        adj_sum = sb("adj_sum", [P, 1])
        adj_off = sb("adj_off", [P, 1])
        found = sb("found", [P, 1])
        scratch = sb("scratch", [P, NT * N])
        bad = sb("bad", [P, 2 * NT + 2])
        bad_n = sb("bad_n", [1, 1], I32)
        rz = sb("rz", [P, NT, 2 * H])
        rh = sb("rh", [P, NT, H])
        pre_n = sb("pre_n", [P, NT, H])
        n_gate = sb("n_gate", [P, NT, H])
        diff = sb("diff", [P, NT, H])
        keep = sb("keep", [P, NT, H])
        y = sb("y", [P, NT, H])
        stats = sb("stats", [P, NT, 6])
        mv = sb("mv", [P, NT, 2])
        rstd = sb("rstd", [P, NT])
        out_sb = sb("out_sb", [P, NT, H])
        warm = sb("warm", [P, 2])
        half = sb("half", [P, 1])
        eps = sb("eps", [P, 1])
        std = sb("std", [P, NT])
        adj_f = sb("adj_f", [P, NT, N])
        table = sb("table", [P, BUFFERS, ROWS_PER_LOAD, NT * H])

        agg_ps = psum("agg_ps", [P, BANK])
        gru_ps = psum("gru_ps", [P, NT, BANK])
        rest_ps = psum("rest_ps", [P, BANKS, BANK])
        base_ps = rest_ps[:, BANKS - 1, BANK - 32:BANK - 32 + NT]
        bad_ps = rest_ps[0:1, BANKS - 1, BANK - 16:BANK - 16 + 2 * NT + 2]
        assert len(groups[-1]) * STRIDE <= BANK - 32 and XR <= STRIDE
        assert BANKS >= BUFFERS + 1

        def chunk_ps(q, a, b):
            o = (q % CHUNKS_PER_BANK) * STRIDE
            return rest_ps[:, q // CHUNKS_PER_BANK, o + a:o + b]

        def group_ps(g, a, b):
            n = len(groups[g])
            return rest_ps[:, g, 0:n * STRIDE].rearrange("p (q c) -> p q c", q=n)[:, :, a:b]

        adj_loaded = [sem(f"adj_loaded{t}") for t in range(NT)]
        x_loaded, xT_loaded, w_loaded, bias_loaded = sem("x_loaded"), sem("xT_loaded"), sem("w_loaded"), sem("bias_loaded")
        key_of_i_ready, index_consts, rank_consts = sem("key_of_i_ready"), sem("index_consts"), sem("rank_consts")
        ones_ready, before_ready, bias_zeroed, ones2_ready = sem("ones_ready"), sem("before_ready"), sem("bias_zeroed"), sem("ones2_ready")
        edge_zeroed, half_ready, warm_ready = sem("edge_zeroed"), sem("half_ready"), sem("warm_ready")
        keys_made, top8_made, keys2_made, lists_made = sem("keys_made"), sem("top8_made"), sem("keys2_made"), sem("lists_made")
        direct_indexed = sem("direct_indexed")
        filled_made, rest_counted, found_copied, bases_made, ends_made = sem("filled_made"), sem("rest_counted"), sem("found_copied"), sem("bases_made"), sem("ends_made")
        x_rest_x, x_rest_ready = sem("x_rest_x"), sem("x_rest_ready")
        before_end_made, rank_hot_made = sem("before_end_made"), sem("rank_hot_made")
        group_compacted, slot_made, slot_eq_made, slot_key_made, rest_key_made = sem("group_compacted"), sem("slot_made"), sem("slot_eq_made"), sem("slot_key_made"), sem("rest_key_made")
        rest_row_made, rest_indexed = sem("rest_row_made"), sem("rest_indexed")
        gathered = [sem(f"gathered{g}") for g in range(GATHERS)]
        prod_made, target_hot_made = sem("prod_made"), sem("target_hot_made")
        adj_summed, bad_made, bad_counted, guard_ready = sem("adj_summed"), sem("bad_made"), sem("bad_counted"), sem("guard_ready")
        agg_summed, aggT_ready, gates_summed = sem("agg_summed"), sem("aggT_ready"), sem("gates_summed")
        rz_made, rh_made, pre_n_made, n_made, diff_made, keep_made = sem("rz_made"), sem("rh_made"), sem("pre_n_made"), sem("n_made"), sem("diff_made"), sem("keep_made")
        y_made, stats_made, mv_made, rstd_made, std_made, out_made, stored = sem("y_made"), sem("stats_made"), sem("mv_made"), sem("rstd_made"), sem("std_made"), sem("out_made"), sem("stored")
        adj_f_made = sem("adj_f_made")
        table_loaded = [sem(f"table_loaded{b}") for b in range(BUFFERS)]
        table_free = [sem(f"table_free{b}") for b in range(BUFFERS)]
        weighted = [sem(f"weighted{b}") for b in range(BUFFERS)]
        rows_summed = [sem(f"rows_summed{b}") for b in range(BUFFERS)]
        rows_free = [sem(f"rows_free{b}") for b in range(BUFFERS)]

        out_rows = out.rearrange("(t p) h -> p t h", p=P)
        table_rows = edge_table.rearrange("(l r t p) h -> l r p t h", r=ROWS_PER_LOAD, t=NT, p=P)
        HALF = NT // 2

        block = ctx.enter_context(nc.Block())

        @block.sync
        def _(sp):
            for t in range(NT):
                sp.dma_start(adj_sb[:, t, :], adj_t[t * P:(t + 1) * P, :]).then_inc(adj_loaded[t], 16)
            sp.dma_start(x_sb[:], x.rearrange("(t p) h -> p t h", p=P)).then_inc(x_loaded, 16)
            sp.wait_ge(guard_ready, 1)
            broken = sp.value_load(bad_n[0:1, 0:1], min_val=0, max_val=1)
            with sp.If(broken != 0):
                with sp.Fori(0, LOADS // BUFFERS) as step:
                    for b in range(BUFFERS):
                        sp.wait_ge(table_free[b], step + 1)
                        for r in range(ROWS_PER_LOAD):
                            src = table_rows[bass.ds(step * BUFFERS + b, 1), r, :, :, :].rearrange("l p t h -> (l p) t h")
                            sp.dma_start(table[:, b, r, :].rearrange("p (t h) -> p t h", t=NT), src).then_inc(table_loaded[b], 16)
            for g in range(2):
                sp.wait_ge(out_made, (g + 1) * HALF)
                sp.dma_start(out_rows[:, g * HALF:(g + 1) * HALF, :], out_sb[:, g * HALF:(g + 1) * HALF, :]).then_inc(stored, 16)
            sp.wait_ge(stored, 32)

        @block.gpsimd
        def _(pool):
            nc.gpsimd.iota(key_of_i[:], [[-1, N]], base=N, channel_multiplier=0,
                           allow_small_or_imprecise_dtypes=True).then_inc(key_of_i_ready, 1)
            nc.gpsimd.iota(flat_of_j[:], [[P, NT]], base=INVALID, channel_multiplier=1,
                           allow_small_or_imprecise_dtypes=True).then_inc(index_consts, 1)
            nc.gpsimd.memset(ones2[:], 1.0).then_inc(ones2_ready, 1)
            nc.gpsimd.memset(ones[:], 1.0).then_inc(ones_ready, 1)
            pool.wait_ge(ones_ready, 1)
            nc.gpsimd.affine_select(out=before[:], in_=ones[:], compare_op=ALU.is_gt, fill=0.0, base=0,
                                    pattern=[[1, P]], channel_multiplier=-1).then_inc(before_ready, 1)
            nc.gpsimd.iota(rank_iota[:], [[1, CHUNKS * P]], base=0, channel_multiplier=0,
                           allow_small_or_imprecise_dtypes=True).then_inc(rank_consts, 1)
            nc.gpsimd.iota(rank_of[:], [[P, CHUNKS]], base=0, channel_multiplier=1,
                           allow_small_or_imprecise_dtypes=True).then_inc(rank_consts, 1)
            nc.gpsimd.iota(slot_iota[:], [[1, REST]], base=0, channel_multiplier=0,
                           allow_small_or_imprecise_dtypes=True).then_inc(rank_consts, 1)
            nc.gpsimd.iota(x_rest[:, :, COL_J], [[P, NT]], base=0, channel_multiplier=1,
                           allow_small_or_imprecise_dtypes=True).then_inc(x_rest_x, 1)
            for t in range(NT):
                nc.gpsimd.memset(low[:, t:t + 1], float(WINDOWS[t][0] * P)).then_inc(rank_consts, 1)
                nc.gpsimd.memset(high[:, t:t + 1], float(WINDOWS[t][1] * P)).then_inc(rank_consts, 1)
            pool.wait_ge(edge_zeroed, 1)
            for t in range(NT):
                pool.wait_ge(direct_indexed, t + 1)
                for s in range(DIRECT):
                    g = t * DIRECT + s
                    nc.gpsimd.indirect_dma_start(
                        out=edge[:, g, :], out_offset=None, in_=edge_table,
                        in_offset=bass.IndirectOffsetOnAxis(ap=idx_direct[:, t, s:s + 1], axis=0),
                        bounds_check=N * N - 1, oob_is_err=False).then_inc(gathered[g], 16)
            for b, qs in enumerate(groups):
                pool.wait_ge(rest_indexed, b + 1)
                for q in qs:
                    g = NT * DIRECT + q
                    nc.gpsimd.indirect_dma_start(
                        out=edge[:, g, :], out_offset=None, in_=edge_table,
                        in_offset=bass.IndirectOffsetOnAxis(ap=idx_rest[:, q:q + 1], axis=0),
                        bounds_check=N * N - 1, oob_is_err=False).then_inc(gathered[g], 16)

        @block.scalar
        def _(act):
            act.dma_start(xT_sb[:], x_t).then_inc(xT_loaded, 16)
            act.dma_start(whh_sb[:], w_hh_t).then_inc(w_loaded, 16)
            act.wait_ge(bias_zeroed, 1)
            act.dma_start(bias2[0:1, 0:G3], b_ih.rearrange("(a g) -> a g", a=1)).then_inc(bias_loaded, 16)
            act.dma_start(bias2[1:2, 0:2 * H], b_hh[0:2 * H].rearrange("(a g) -> a g", a=1)).then_inc(bias_loaded, 16)
            act.dma_start(bias2[1:2, G3:G3 + H], b_hh[2 * H:G3].rearrange("(a g) -> a g", a=1)).then_inc(bias_loaded, 16)
            act.dma_start(wih_sb[:], w_ih_t).then_inc(w_loaded, 16)
            act.wait_ge(half_ready, 2)
            nc.scalar.activation(warm[:, 0:1], half[:], ACT.Sigmoid).then_inc(warm_ready, 1)
            for t in range(NT):
                act.wait_ge(adj_loaded[t], 16)
            adj_all = adj_sb[:].rearrange("p t i -> p (t i)")
            nc.scalar.activation(scratch[:], adj_all, ACT.Identity, accum_out=adj_sum[:]).then_inc(adj_summed, 1)
            act.wait_ge(adj_summed, 1)
            nc.scalar.activation(scratch[:], adj_all, ACT.Square, bias=half[:], accum_out=adj_off[:]).then_inc(adj_summed, 1)
            act.wait_ge(x_loaded, 16)
            nc.scalar.copy(x_rest[:, :, 0:H], x_sb[:]).then_inc(x_rest_x, 1)
            act.wait_ge(guard_ready, 1)
            broken = act.value_load(bad_n[0:1, 0:1], min_val=0, max_val=1)
            act.wait_ge(agg_summed, 1)
            with act.If(broken == 0):
                for t in range(NT):
                    nc.scalar.copy(aggT[:, t * P:(t + 1) * P], agg_ps[:, t * P:(t + 1) * P]).then_inc(aggT_ready, 1)
            with act.Else():
                with act.Fori(0, LOADS // BUFFERS) as step:
                    for b in range(BUFFERS):
                        act.wait_ge(rows_summed[b], step + 1)
                        nc.scalar.copy(aggT[:, bass.ds((step * BUFFERS + b) * ROWS_PER_LOAD, ROWS_PER_LOAD)],
                                       rest_ps[:, b, 0:ROWS_PER_LOAD]).then_inc(rows_free[b], 1)
                for b in range(BUFFERS):
                    act.wait_ge(rows_free[b], LOADS // BUFFERS + 1)
                nc.scalar.copy(warm[:, 1:2], half[:]).then_inc(aggT_ready, NT)
            for g in range(2):
                for t in range(g * HALF, (g + 1) * HALF):
                    act.wait_ge(gates_summed, t + 1)
                    nc.scalar.activation(rz[:, t, :], gru_ps[:, t, 0:2 * H], ACT.Sigmoid).then_inc(rz_made, 1)
                act.wait_ge(pre_n_made, g + 1)
                nc.scalar.activation(n_gate[:, g * HALF:(g + 1) * HALF, :], pre_n[:, g * HALF:(g + 1) * HALF, :],
                                     ACT.Tanh).then_inc(n_made, 1)
            nc.scalar.activation(warm[:, 0:1], eps[:], ACT.Sqrt).then_inc(warm_ready, 1)
            act.wait_ge(mv_made, NT)
            nc.scalar.activation(std[:], mv[:, :, 1], ACT.Sqrt, bias=eps[:]).then_inc(std_made, 1)

        @block.tensor
        def _(pe):
            pe.wait_ge(ones2_ready, 1)
            pe.wait_ge(bias_loaded, 48)
            pe.wait_ge(xT_loaded, 16)
            pe.wait_ge(w_loaded, 32)
            for t in range(NT):
                nc.tensor.matmul(gru_ps[:, t, :], ones2[:], bias2[:], start=True, stop=False, skip_group_check=True)
                lhs = xT_sb[:, t * P:(t + 1) * P]
                nc.tensor.matmul(gru_ps[:, t, 0:2 * H], lhs, whh_sb[:, 0:2 * H], start=False, stop=False, skip_group_check=True)
                nc.tensor.matmul(gru_ps[:, t, G3:G3 + H], lhs, whh_sb[:, 2 * H:G3], start=False, stop=False, skip_group_check=True)

            pe.wait_ge(before_ready, 1)
            pe.wait_ge(rest_counted, 1)
            nc.tensor.matmul(base_ps, before[:], rest_n[:], start=True, stop=False, skip_group_check=True)
            for k in range(1, NT):
                mm = nc.tensor.matmul(base_ps[:, k:NT], ones[:], rest_n[:, 0:NT - k], start=False, stop=(k == NT - 1), skip_group_check=True)
            mm.then_inc(bases_made, 1)
            pe.wait_ge(bad_made, 4)
            nc.tensor.matmul(bad_ps, ones[:, 0:1], bad[:], start=False, stop=True, skip_group_check=True).then_inc(bad_counted, 1)

            pe.wait_ge(x_rest_ready, 1)
            for b, qs in enumerate(groups):
                if b == BANKS - 1:
                    pe.wait_ge(guard_ready, 1)
                    pe.wait_ge(ends_made, 1)
                for q in qs:
                    tiles = [t for t in range(NT) if WINDOWS[t][0] <= q < WINDOWS[t][1]]
                    pe.wait_ge(rank_hot_made, tiles[-1] + 1)
                    for t in tiles:
                        o = (q - WINDOWS[t][0]) * P
                        mm = nc.tensor.matmul(chunk_ps(q, 0, XR), rank_hot[:, t, o:o + P], x_rest[:, t, :],
                                              start=(t == tiles[0]), stop=(t == tiles[-1]))
                mm.then_inc(group_compacted, 1)

            for g in range(GATHERS):
                pe.wait_ge(target_hot_made, g + 1)
                pe.wait_ge(prod_made, g // DIRECT + 1 if g < NT * DIRECT else NT + g - NT * DIRECT + 1)
                mm = nc.tensor.matmul(agg_ps[:], prod[:, g, :], target_hot[:, g, :],
                                      start=(g == 0), stop=(g == GATHERS - 1))
            mm.then_inc(agg_summed, 1)

            pe.wait_ge(guard_ready, 1)
            broken = pe.value_load(bad_n[0:1, 0:1], min_val=0, max_val=1)
            with pe.If(broken != 0):
                pe.wait_ge(adj_f_made, 1)
                with pe.Fori(0, LOADS // BUFFERS) as step:
                    for b in range(BUFFERS):
                        pe.wait_ge(weighted[b], step + 1)
                        pe.wait_ge(rows_free[b], step + 1)
                        for r in range(ROWS_PER_LOAD):
                            for t in range(NT):
                                i = (step * BUFFERS + b) * ROWS_PER_LOAD + r
                                mm = nc.tensor.matmul(rest_ps[:, b, r:r + 1], table[:, b, r, t * H:(t + 1) * H],
                                                      adj_f[:, t, bass.ds(i, 1)], start=(t == 0), stop=(t == NT - 1))
                        mm.then_inc(rows_summed[b], 1)
                        nc.tensor.matmul(rest_ps[0:1, BUFFERS, 0:1], ones[:, 0:1], ones[:, 0:1], start=True, stop=True).then_inc(table_free[b], 1)
            for t in range(NT):
                pe.wait_ge(aggT_ready, t + 1)
                nc.tensor.matmul(gru_ps[:, t, 0:G3], aggT[:, t * P:(t + 1) * P], wih_sb[:], start=False, stop=True,
                                 skip_group_check=True).then_inc(gates_summed, 1)

        @block.vector
        def _(dve):
            nc.vector.memset(bias2[:], 0.0).then_inc(bias_zeroed, 1)
            nc.vector.memset(eps[:], EPS).then_inc(half_ready, 1)
            nc.vector.memset(half[:], -0.5).then_inc(half_ready, 1)
            nc.vector.memset(edge[:], 0.0).then_inc(edge_zeroed, 1)

            def list_top(t):
                dve.wait_ge(adj_loaded[t], 16)
                nc.vector.tensor_tensor(keys[:, t, :], adj_sb[:, t, :], key_of_i[:], ALU.mult).then_inc(keys_made, 1)
                dve.wait_ge(keys_made, t + 1)
                nc.vector.max(lists[:, t, 0:8], keys[:, t, :]).then_inc(top8_made, 1)
                dve.wait_ge(top8_made, t + 1)
                nc.vector.tensor_scalar(idx_direct[:, t, :], lists[:, t, 0:DIRECT], float(-N), flat_of_j[:, t:t + 1],
                                        ALU.mult, ALU.add).then_inc(direct_indexed, 1)

            def list_next(t):
                nc.vector.match_replace(keys2[:, t, :], lists[:, t, 0:8], keys[:, t, :], 0.0).then_inc(keys2_made, 1)
                dve.wait_ge(keys2_made, t + 1)
                nc.vector.max(lists[:, t, 8:16], keys2[:, t, :]).then_inc(lists_made, 1)

            def targets(g, key):
                nc.vector.tensor_scalar(target_hot[:, g, :], key_of_i[:], key, None, ALU.is_equal).then_inc(target_hot_made, 1)

            dve.wait_ge(key_of_i_ready, 1)
            dve.wait_ge(index_consts, 1)
            list_top(0)
            list_top(1)
            list_next(0)
            list_next(1)
            list_top(2)
            list_top(3)
            list_next(2)
            list_next(3)

            dve.wait_ge(lists_made, NT)
            nc.vector.tensor_scalar(filled[:], lists[:], 0.0, None, ALU.is_gt).then_inc(filled_made, 1)
            dve.wait_ge(filled_made, 1)
            nc.vector.tensor_reduce(rest_n[:], filled[:, :, DIRECT:SLOTS], AX.X, ALU.add).then_inc(rest_counted, 1)
            nc.vector.tensor_reduce(found[:], filled[:], AX.XY, ALU.add).then_inc(found_copied, 1)
            nc.vector.tensor_copy(x_rest[:, :, COL_LIST:COL_LIST + REST], lists[:, :, DIRECT:SLOTS]).then_inc(x_rest_x, 1)
            dve.wait_ge(bases_made, 1)
            dve.wait_ge(x_rest_x, 3)
            nc.vector.tensor_tensor(rest_end[:], base_ps, rest_n[:], ALU.add).then_inc(ends_made, 1)
            nc.vector.tensor_copy(x_rest[:, :, COL_BASE], base_ps).then_inc(x_rest_ready, 1)
            dve.wait_ge(ends_made, 1)
            dve.wait_ge(x_rest_ready, 1)
            dve.wait_ge(rank_consts, 3 + 2 * NT)
            for t, (a, b) in enumerate(WINDOWS):
                w = (b - a) * P
                nc.vector.tensor_scalar(is_before_end[:, t, 0:w], rank_iota[:, a * P:b * P], rest_end[:, t:t + 1], None,
                                        ALU.is_lt).then_inc(before_end_made, 1)
                dve.wait_ge(before_end_made, t + 1)
                nc.vector.scalar_tensor_tensor(out=rank_hot[:, t, 0:w], in0=rank_iota[:, a * P:b * P],
                                               scalar=x_rest[:, t, COL_BASE:COL_BASE + 1], in1=is_before_end[:, t, 0:w],
                                               op0=ALU.is_ge, op1=ALU.mult).then_inc(rank_hot_made, 1)
            dve.wait_ge(adj_summed, 2)
            dve.wait_ge(found_copied, 1)
            nc.vector.tensor_tensor(bad[:, 0:NT], x_rest[:, :, COL_BASE], low[:], ALU.is_lt).then_inc(bad_made, 1)
            nc.vector.tensor_tensor(bad[:, NT:2 * NT], rest_end[:], high[:], ALU.is_gt).then_inc(bad_made, 1)
            nc.vector.tensor_tensor(bad[:, 2 * NT:2 * NT + 1], adj_sum[:], found[:], ALU.not_equal).then_inc(bad_made, 1)
            nc.vector.tensor_scalar(bad[:, 2 * NT + 1:2 * NT + 2], adj_off[:], N * NT / 4, None, ALU.not_equal).then_inc(bad_made, 1)
            dve.wait_ge(bad_counted, 1)
            nc.vector.tensor_reduce(bad_n[:], bad_ps, AX.X, ALU.max).then_inc(guard_ready, 1)

            def rest_index(b):
                qs = slice(groups[b][0], groups[b][-1] + 1)
                n = len(groups[b])
                dve.wait_ge(group_compacted, b + 1)
                nc.vector.tensor_tensor(slot_of[:, qs], rank_of[:, qs],
                                        group_ps(b, COL_BASE, COL_BASE + 1).rearrange("p q c -> p (q c)"), ALU.subtract).then_inc(slot_made, 1)
                dve.wait_ge(slot_made, b + 1)
                nc.vector.tensor_tensor(slot_eq[:, qs, :], slot_iota[:].unsqueeze(1).to_broadcast([P, n, REST]),
                                        slot_of[:, qs].unsqueeze(2).to_broadcast([P, n, REST]), ALU.is_equal).then_inc(slot_eq_made, 1)
                dve.wait_ge(slot_eq_made, b + 1)
                nc.vector.tensor_tensor(slot_key[:, qs, :], slot_eq[:, qs, :], group_ps(b, COL_LIST, COL_LIST + REST), ALU.mult).then_inc(slot_key_made, 1)
                dve.wait_ge(slot_key_made, b + 1)
                nc.vector.tensor_reduce(rest_key[:, qs], slot_key[:, qs, :], AX.X, ALU.add).then_inc(rest_key_made, 1)
                dve.wait_ge(rest_key_made, b + 1)
                nc.vector.tensor_scalar(rest_row[:, qs], rest_key[:, qs], float(-N), float(INVALID), ALU.mult, ALU.add).then_inc(rest_row_made, 1)
                dve.wait_ge(rest_row_made, b + 1)
                nc.vector.tensor_tensor(idx_rest[:, qs], rest_row[:, qs],
                                        group_ps(b, COL_J, COL_J + 1).rearrange("p q c -> p (q c)"), ALU.add).then_inc(rest_indexed, 1)

            for b in range(BANKS):
                rest_index(b)

            dve.wait_ge(x_loaded, 16)
            for t in range(NT):
                for s in range(DIRECT):
                    targets(t * DIRECT + s, lists[:, t, s:s + 1])
                for s in range(DIRECT):
                    dve.wait_ge(gathered[t * DIRECT + s], 16)
                nc.vector.tensor_tensor(prod[:, t * DIRECT:(t + 1) * DIRECT, :], edge[:, t * DIRECT:(t + 1) * DIRECT, :],
                                        x_sb[:, t:t + 1, :].to_broadcast([P, DIRECT, H]), ALU.mult).then_inc(prod_made, 1)
            for q in range(CHUNKS):
                g = NT * DIRECT + q
                targets(g, rest_key[:, q:q + 1])
                dve.wait_ge(gathered[g], 16)
                nc.vector.tensor_tensor(prod[:, g, :], edge[:, g, :], chunk_ps(q, 0, H), ALU.mult).then_inc(prod_made, 1)

            broken = dve.value_load(bad_n[0:1, 0:1], min_val=0, max_val=1)
            with dve.If(broken != 0):
                nc.vector.tensor_copy(adj_f[:], adj_sb[:]).then_inc(adj_f_made, 1)
                for b in range(BUFFERS):
                    nc.vector.memset(warm[:, 1:2], 0.0).then_inc(table_free[b], 1)
                    nc.vector.memset(warm[:, 1:2], 0.0).then_inc(rows_free[b], 1)
                with dve.Fori(0, LOADS // BUFFERS) as step:
                    for b in range(BUFFERS):
                        dve.wait_ge(table_loaded[b], (step + 1) * (16 * ROWS_PER_LOAD))
                        nc.vector.tensor_tensor(table[:, b], table[:, b],
                                                x_sb[:].rearrange("p t h -> p (t h)").unsqueeze(1).to_broadcast([P, ROWS_PER_LOAD, NT * H]),
                                                ALU.mult).then_inc(weighted[b], 1)

            for g in range(2):
                s = slice(g * HALF, (g + 1) * HALF)
                dve.wait_ge(rz_made, (g + 1) * HALF)
                nc.vector.tensor_tensor(rh[:, s, :], rz[:, s, 0:H], gru_ps[:, s, G3:G3 + H], ALU.mult).then_inc(rh_made, 1)
                dve.wait_ge(rh_made, g + 1)
                nc.vector.tensor_tensor(pre_n[:, s, :], rh[:, s, :], gru_ps[:, s, 2 * H:G3], ALU.add).then_inc(pre_n_made, 1)
            for g in range(2):
                s = slice(g * HALF, (g + 1) * HALF)
                dve.wait_ge(n_made, g + 1)
                nc.vector.tensor_tensor(diff[:, s, :], x_sb[:, s, :], n_gate[:, s, :], ALU.subtract).then_inc(diff_made, 1)
                dve.wait_ge(diff_made, g + 1)
                nc.vector.scalar_tensor_tensor(out=keep[:, s, :], in0=rz[:, s, H:2 * H], scalar=-1.0, in1=diff[:, s, :],
                                               op0=ALU.add, op1=ALU.mult).then_inc(keep_made, 1)
                dve.wait_ge(keep_made, g + 1)
                nc.vector.scalar_tensor_tensor(out=y[:, s, :], in0=x_sb[:, s, :], scalar=2.0, in1=keep[:, s, :],
                                               op0=ALU.mult, op1=ALU.add).then_inc(y_made, 1)
                dve.wait_ge(y_made, g + 1)
                for t in range(g * HALF, (g + 1) * HALF):
                    nc.vector.bn_stats(stats[:, t, :], y[:, t, :]).then_inc(stats_made, 1)
                for t in range(g * HALF, (g + 1) * HALF):
                    dve.wait_ge(stats_made, t + 1)
                    nc.vector.bn_aggr(mv[:, t, :], stats[:, t, :]).then_inc(mv_made, 1)
            dve.wait_ge(std_made, 1)
            nc.vector.reciprocal(rstd[:], std[:]).then_inc(rstd_made, 1)
            dve.wait_ge(rstd_made, 1)
            for t in range(NT):
                nc.vector.tensor_scalar(out_sb[:, t, :], y[:, t, :], mv[:, t, 0:1], rstd[:, t:t + 1],
                                        ALU.subtract, ALU.mult).then_inc(out_made, 1)


def kernel(x, adj, L0_gnn_edge_table, L0_gnn_w_ih, L0_gnn_w_hh, L0_gnn_b_ih, L0_gnn_b_hh):
    import numpy as np
    import concourse.bacc as bacc
    from concourse.bass_utils import run_bass_kernel_spmd

    x, adj, w_ih, w_hh = (np.asarray(a) for a in (x, adj, L0_gnn_w_ih, L0_gnn_w_hh))
    arrays = {
        "x": np.ascontiguousarray(x),
        "x_t": np.ascontiguousarray(x.T),
        "adj_t": np.ascontiguousarray(adj.T),
        "edge_table": np.ascontiguousarray(L0_gnn_edge_table),
        "w_ih_t": np.ascontiguousarray(w_ih.T),
        "w_hh_t": np.ascontiguousarray(w_hh.T),
        "b_ih": np.ascontiguousarray(L0_gnn_b_ih),
        "b_hh": np.ascontiguousarray(L0_gnn_b_hh),
    }
    nc = bacc.Bacc("TRN2", target_bir_lowering=False, num_devices=1)
    args = [nc.dram_tensor(name, a.shape, mybir.dt.from_np(a.dtype), kind="ExternalInput").ap()
            for name, a in arrays.items()]
    out = nc.dram_tensor("out", x.shape, F32, kind="ExternalOutput").ap()
    gnn_gru_norm(nc, *args, out)
    r = run_bass_kernel_spmd(nc, [arrays], core_ids=[0])
    return r.results[0]["out"]
```

```python
from contextlib import ExitStack

import concourse.bass as bass
from concourse import mybir

F32 = mybir.dt.float32
F32R = mybir.dt.float32r
F16 = mybir.dt.float16
BF16 = mybir.dt.bfloat16
I32 = mybir.dt.int32
ALU = mybir.AluOpType
ACT = mybir.ActivationFunctionType
AX = mybir.AxisListType

P = 128
TOP = 8
SLOTS = 2 * TOP
EDGE = 1024.0
DIRECT = 3
REST = SLOTS - DIRECT
WINDOWS = ((0, 2), (0, 4), (1, 5), (3, 7))
CHUNKS = WINDOWS[-1][1]
CHUNKS_PER_BANK = 3
BANK = 512
ROWS_PER_LOAD = 4
BUFFERS = 2
WARM_UP = 7
ACT_TARGETS = 6
EPS = 1e-5


def gnn_gru_norm(nc, x, x_t, adj_t, edge_table, w_ih_t, w_hh_t, b_ih, b_hh, out):
    N, H = x.shape
    NT = N // P
    G3 = 3 * H
    INVALID = N * N
    GATHERS = NT * DIRECT + CHUNKS
    XR = H + REST + 2
    COL_LIST, COL_BASE, COL_J = H, H + REST, H + REST + 1
    STRIDE = BANK // CHUNKS_PER_BANK
    BANKS = -(-CHUNKS // CHUNKS_PER_BANK)
    groups = [range(b * CHUNKS_PER_BANK, min((b + 1) * CHUNKS_PER_BANK, CHUNKS)) for b in range(BANKS)]
    BAD = 3 * NT + 1
    LOADS = N // ROWS_PER_LOAD

    with ExitStack() as ctx:
        def sb(name, shape, dt=F32):
            return ctx.enter_context(nc.sbuf_tensor(name, shape, dt))

        def psum(name, shape):
            return ctx.enter_context(nc.psum_tensor(name, shape, F32))

        def sem(name):
            return ctx.enter_context(nc.semaphore(name))

        adj_sb = sb("adj_sb", [P, NT, N], I32)
        x_sb = sb("x_sb", [P, NT, H])
        xT_sb = sb("xT_sb", [P, N])
        wih_sb = sb("wih_sb", [P, G3])
        whh_sb = sb("whh_sb", [P, G3])
        bias2 = sb("bias2", [P, BANK])
        bias_high = sb("bias_high", [P, BANK], F32R)
        bias_low = sb("bias_low", [P, BANK], F32R)
        key_of_i = sb("key_of_i", [P, N])
        row_first = sb("row_first", [P, N], F16)
        row_last = sb("row_last", [P, N], F16)
        ones16 = sb("ones16", [P, P], F16)
        take_row0 = sb("take_row0", [P, P], F16)
        rows01 = sb("rows01", [P, P])
        take_rows01 = sb("take_rows01", [P, P], F32R)
        edge_diag = sb("edge_diag", [P, P], F16)
        minus_edge = sb("minus_edge", [P, 1])
        edge_n_1 = sb("edge_n_1", [P, 1])
        rank_odd = sb("rank_odd", [P, CHUNKS * P])
        rank_of = sb("rank_of", [P, CHUNKS])
        slot_iota = sb("slot_iota", [P, REST])
        flat_of_j = sb("flat_of_j", [P, NT])
        before = sb("before", [P, P], F16)
        ones = sb("ones", [P, P])
        low = sb("low", [P, NT])
        high = sb("high", [P, NT])
        adj16 = sb("adj16", [P, NT, N], F16)
        keys0 = sb("keys0", [P, N])
        lists = sb("lists", [P, NT, SLOTS])
        last = sb("last", [P, NT, TOP])
        last_key = sb("last_key", [P, NT, TOP])
        is_new = sb("is_new", [P, NT, TOP])
        filled = sb("filled", [P, NT, SLOTS])
        idx_direct = sb("idx_direct", [P, NT, DIRECT], I32)
        rest_n = sb("rest_n", [P, NT])
        rest_n16 = sb("rest_n16", [P, NT], F16)
        rest_end = sb("rest_end", [P, NT])
        x_rest = sb("x_rest", [P, NT, XR])
        j_of = sb("j_of", [P, NT])
        base = sb("base", [P, NT])
        minus_mid = sb("minus_mid", [P, NT])
        half_sq = sb("half_sq", [P, NT])
        off_sq = sb("off_sq", [P, NT, 4 * P])
        rank_hot = sb("rank_hot", [P, NT, 4 * P])
        slot_of = sb("slot_of", [P, CHUNKS])
        flat_of_c = sb("flat_of_c", [P, CHUNKS])
        slot_key = sb("slot_key", [P, CHUNKS, REST])
        rest_key = sb("rest_key", [P, CHUNKS])
        idx_rest = sb("idx_rest", [P, CHUNKS], I32)
        edge = sb("edge", [P, GATHERS, H])
        prod = sb("prod", [P, GATHERS, H])
        high_part = sb("high_part", [P, NT * DIRECT, H], F32R)
        low_part = sb("low_part", [P, NT * DIRECT, H], F32R)
        off_i = sb("off_i", [P, ACT_TARGETS, N])
        direct_hot = sb("direct_hot", [P, NT * DIRECT, N], F32R)
        rest_hot = sb("rest_hot", [P, CHUNKS, N])
        aggT = sb("aggT", [P, N])
        adj_sum = sb("adj_sum", [P, NT])
        adj_off = sb("adj_off", [P, 1])
        found = sb("found", [P, NT])
        scratch = sb("scratch", [P, NT * N])
        bad = sb("bad", [P, BAD])
        bad_n = sb("bad_n", [1, 1], I32)
        rz = sb("rz", [P, NT, 2 * H])
        rh = sb("rh", [P, NT, H])
        pre_n = sb("pre_n", [P, NT, H])
        n_gate = sb("n_gate", [P, NT, H])
        zx = sb("zx", [P, NT, H])
        x_part = sb("x_part", [P, NT, H])
        n_part = sb("n_part", [P, NT, H])
        y = sb("y", [P, NT, H])
        stats = sb("stats", [P, NT, 6])
        mv = sb("mv", [P, NT, 2])
        rstd = sb("rstd", [P, NT])
        shift = sb("shift", [P, NT])
        out_sb = sb("out_sb", [P, NT, H])
        warm = sb("warm", [P, 2])
        credit = sb("credit", [P, 2 * BUFFERS])
        half = sb("half", [P, 1])
        eps = sb("eps", [P, 1])
        std = sb("std", [P, NT])
        adj_f = sb("adj_f", [P, NT, N])
        table = sb("table", [P, BUFFERS, ROWS_PER_LOAD, NT * H])

        agg_ps = psum("agg_ps", [P, BANK])
        gru_ps = psum("gru_ps", [P, NT, BANK])
        rest_ps = psum("rest_ps", [P, BANKS, BANK])
        base_ps = rest_ps[:, BANKS - 1, BANK - 32:BANK - 32 + NT]
        bad_ps = rest_ps[0:1, BANKS - 1, BANK - 16:BANK - 16 + BAD]
        first_ps = [None] + [gru_ps[:, t, :] for t in range(1, NT)]
        last_ps = [agg_ps[:]] + [rest_ps[:, t, :] for t in range(NT - 1)]
        assert len(groups[-1]) * STRIDE <= BANK - 32 and XR <= STRIDE
        assert BANKS >= BUFFERS + 1

        def chunk_ps(q, a, b):
            o = (q % CHUNKS_PER_BANK) * STRIDE
            return rest_ps[:, q // CHUNKS_PER_BANK, o + a:o + b]

        def group_ps(g, a, b):
            n = len(groups[g])
            return rest_ps[:, g, 0:n * STRIDE].rearrange("p (q c) -> p q c", q=n)[:, :, a:b]

        adj_loaded = [sem(f"adj_loaded{t}") for t in range(NT)]
        x_loaded, xT_loaded, w_loaded, bias_loaded = sem("x_loaded"), sem("xT_loaded"), sem("w_loaded"), sem("bias_loaded")
        take_rows_rounded, bias_high_made, bias_low_made, rest_rounded, j_ready = (
            sem("take_rows_rounded"), sem("bias_high_made"), sem("bias_low_made"), sem("rest_rounded"), sem("j_ready"))
        wih_loaded, key_of_i_ready, index_consts, rank_consts, edge_diag_ready = (
            sem("wih_loaded"), sem("key_of_i_ready"), sem("index_consts"), sem("rank_consts"), sem("edge_diag_ready"))
        rows_ready, ones_ready, before_ready, bias_zeroed, ones2_ready = (
            sem("rows_ready"), sem("ones_ready"), sem("before_ready"), sem("bias_zeroed"), sem("ones2_ready"))
        edge_zeroed, scalars_ready, warm_ready, adj16_made, keys0_made = (
            sem("edge_zeroed"), sem("scalars_ready"), sem("warm_ready"), sem("adj16_made"), sem("keys0_made"))
        keys_summed, first_made, last_made, direct_indexed, last_key_made = (
            sem("keys_summed"), sem("first_made"), sem("last_made"), sem("direct_indexed"), sem("last_key_made"))
        is_new_made, lists_made, filled_made, rest_counted, found_counted = (
            sem("is_new_made"), sem("lists_made"), sem("filled_made"), sem("rest_counted"), sem("found_counted"))
        listed, bases_summed, base_made, mid_made, half_sq_made = (
            sem("listed"), sem("bases_summed"), sem("base_made"), sem("mid_made"), sem("half_sq_made"))
        off_sq_made, x_rest_ready, rank_hot_made, group_compacted, slot_made = (
            sem("off_sq_made"), sem("x_rest_ready"), sem("rank_hot_made"), sem("group_compacted"), sem("slot_made"))
        slot_key_made, rest_indexed, prod_made, high_made, low_made = (
            sem("slot_key_made"), sem("rest_indexed"), sem("prod_made"), sem("high_made"), sem("low_made"))
        off_i_made, direct_hot_act, direct_hot_dve, rest_hot_made, adj_off_made = (
            sem("off_i_made"), sem("direct_hot_act"), sem("direct_hot_dve"), sem("rest_hot_made"), sem("adj_off_made"))
        bad_made, bad_counted, guard_ready, rest_end_made, agg_summed = (
            sem("bad_made"), sem("bad_counted"), sem("guard_ready"), sem("rest_end_made"), sem("agg_summed"))
        aggT_ready, gates_summed, rz_made, rh_made, pre_n_made = (
            sem("aggT_ready"), sem("gates_summed"), sem("rz_made"), sem("rh_made"), sem("pre_n_made"))
        n_made, zx_made, x_part_made, n_part_made, y_made = (
            sem("n_made"), sem("zx_made"), sem("x_part_made"), sem("n_part_made"), sem("y_made"))
        stats_made, mv_made, rstd_made, std_made, shift_made = (
            sem("stats_made"), sem("mv_made"), sem("rstd_made"), sem("std_made"), sem("shift_made"))
        out_made, out_made_act, stored = (
            sem("out_made"), sem("out_made_act"), sem("stored"))
        gathered = [sem(f"gathered{g}") for g in range(GATHERS)]
        adj_f_made = sem("adj_f_made")
        table_loaded = [sem(f"table_loaded{b}") for b in range(BUFFERS)]
        table_free = [sem(f"table_free{b}") for b in range(BUFFERS)]
        weighted = [sem(f"weighted{b}") for b in range(BUFFERS)]
        rows_summed = [sem(f"rows_summed{b}") for b in range(BUFFERS)]
        rows_free = [sem(f"rows_free{b}") for b in range(BUFFERS)]

        out_rows = out.rearrange("(t p) h -> p t h", p=P)
        table_rows = edge_table.rearrange("(l r t p) h -> l r p t h", r=ROWS_PER_LOAD, t=NT, p=P)
        HALF = NT // 2

        block = ctx.enter_context(nc.Block())

        @block.sync
        def _(sp):
            for t in range(NT):
                sp.dma_start(adj_sb[:, t, :], adj_t[t * P:(t + 1) * P, :]).then_inc(adj_loaded[t], 16)
            sp.dma_start(xT_sb[:], x_t).then_inc(xT_loaded, 16)
            sp.dma_start(whh_sb[:], w_hh_t).then_inc(w_loaded, 16)
            sp.wait_ge(bias_zeroed, 1)
            sp.dma_start(bias2[0:1, 0:G3], b_ih.rearrange("(a g) -> a g", a=1)).then_inc(bias_loaded, 16)
            sp.dma_start(bias2[1:2, 0:2 * H], b_hh[0:2 * H].rearrange("(a g) -> a g", a=1)).then_inc(bias_loaded, 16)
            sp.dma_start(bias2[1:2, G3:G3 + H], b_hh[2 * H:G3].rearrange("(a g) -> a g", a=1)).then_inc(bias_loaded, 16)
            sp.dma_start(x_sb[:], x.rearrange("(t p) h -> p t h", p=P)).then_inc(x_loaded, 16)
            sp.dma_start(wih_sb[:], w_ih_t).then_inc(wih_loaded, 16)
            sp.wait_ge(guard_ready, 1)
            broken = sp.value_load(bad_n[0:1, 0:1], min_val=0, max_val=P)
            with sp.If(broken != 0):
                with sp.Fori(0, LOADS // BUFFERS) as step:
                    for b in range(BUFFERS):
                        sp.wait_ge(table_free[b], step + 1)
                        for r in range(ROWS_PER_LOAD):
                            src = table_rows[bass.ds(step * BUFFERS + b, 1), r, :, :, :].rearrange("l p t h -> (l p) t h")
                            sp.dma_start(table[:, b, r, :].rearrange("p (t h) -> p t h", t=NT), src).then_inc(table_loaded[b], 16)
            sp.wait_ge(out_made, HALF)
            sp.dma_start(out_rows[:, 0:HALF, :], out_sb[:, 0:HALF, :]).then_inc(stored, 16)
            sp.wait_ge(stored, 32)

        @block.gpsimd
        def _(pool):
            nc.gpsimd.iota(key_of_i[:], [[-1, N]], base=N + int(EDGE), channel_multiplier=0,
                           allow_small_or_imprecise_dtypes=True).then_inc(key_of_i_ready, 1)
            nc.gpsimd.memset(ones[:], 1.0).then_inc(ones_ready, 1)
            nc.gpsimd.memset(edge_diag[:], 0.0).then_inc(ones_ready, 1)
            nc.gpsimd.memset(ones16[:], 1.0).then_inc(ones_ready, 1)
            pool.wait_ge(ones_ready, 3)
            nc.gpsimd.affine_select(out=edge_diag[:], in_=edge_diag[:], compare_op=ALU.not_equal, fill=EDGE, base=0,
                                    pattern=[[1, P]], channel_multiplier=-1).then_inc(edge_diag_ready, 1)
            nc.gpsimd.affine_select(out=take_row0[:], in_=ones16[:], compare_op=ALU.is_gt, fill=0.0, base=1,
                                    pattern=[[0, P]], channel_multiplier=-1).then_inc(edge_diag_ready, 1)
            nc.gpsimd.iota(flat_of_j[:], [[P, NT]], base=INVALID + int(EDGE) * N, channel_multiplier=1,
                           allow_small_or_imprecise_dtypes=True).then_inc(index_consts, 1)
            nc.gpsimd.affine_select(out=rows01[:], in_=ones[:], compare_op=ALU.is_gt, fill=0.0, base=2,
                                    pattern=[[0, P]], channel_multiplier=-1).then_inc(ones2_ready, 1)
            nc.gpsimd.memset(bias2[:], 0.0).then_inc(bias_zeroed, 1)
            nc.gpsimd.affine_select(out=before[:], in_=ones16[:], compare_op=ALU.is_gt, fill=0.0, base=0,
                                    pattern=[[1, P]], channel_multiplier=-1).then_inc(before_ready, 1)
            nc.gpsimd.iota(rank_odd[:], [[2, CHUNKS * P]], base=1, channel_multiplier=0,
                           allow_small_or_imprecise_dtypes=True).then_inc(rank_consts, 1)
            nc.gpsimd.iota(rank_of[:], [[P, CHUNKS]], base=0, channel_multiplier=1,
                           allow_small_or_imprecise_dtypes=True).then_inc(rank_consts, 1)
            nc.gpsimd.iota(slot_iota[:], [[1, REST]], base=0, channel_multiplier=0,
                           allow_small_or_imprecise_dtypes=True).then_inc(rank_consts, 1)
            nc.gpsimd.iota(j_of[:], [[P, NT]], base=0, channel_multiplier=1,
                           allow_small_or_imprecise_dtypes=True).then_inc(j_ready, 1)
            for t in range(NT):
                nc.gpsimd.memset(low[:, t:t + 1], float(WINDOWS[t][0] * P)).then_inc(rank_consts, 1)
                nc.gpsimd.memset(high[:, t:t + 1], float(WINDOWS[t][1] * P)).then_inc(rank_consts, 1)
            pool.wait_ge(edge_zeroed, 1)
            for t in range(NT):
                pool.wait_ge(direct_indexed, t + 1)
                for s in range(DIRECT):
                    g = t * DIRECT + s
                    nc.gpsimd.indirect_dma_start(
                        out=edge[:, g, :], out_offset=None, in_=edge_table,
                        in_offset=bass.IndirectOffsetOnAxis(ap=idx_direct[:, t, s:s + 1], axis=0),
                        bounds_check=N * N - 1, oob_is_err=False).then_inc(gathered[g], 16)
            for b, qs in enumerate(groups):
                pool.wait_ge(rest_indexed, b + 1)
                for q in qs:
                    g = NT * DIRECT + q
                    nc.gpsimd.indirect_dma_start(
                        out=edge[:, g, :], out_offset=None, in_=edge_table,
                        in_offset=bass.IndirectOffsetOnAxis(ap=idx_rest[:, q:q + 1], axis=0),
                        bounds_check=N * N - 1, oob_is_err=False).then_inc(gathered[g], 16)
            for t in range(NT):
                pool.wait_ge(rz_made, t + 1)
                nc.gpsimd.tensor_tensor(zx[:, t, :], rz[:, t, H:2 * H], x_sb[:, t, :], ALU.mult).then_inc(zx_made, 1)
                pool.wait_ge(zx_made, t + 1)
                nc.gpsimd.tensor_tensor(x_part[:, t, :], zx[:, t, :], x_sb[:, t, :], ALU.add).then_inc(x_part_made, 1)

        @block.scalar
        def _(act):
            act.wait_ge(scalars_ready, 4)
            nc.scalar.activation(warm[:, 0:1], half[:], ACT.Sigmoid).then_inc(warm_ready, 1)
            act.wait_ge(key_of_i_ready, 1)
            nc.scalar.activation(row_last[:], key_of_i[:], ACT.Identity, scale=-1.0, bias=edge_n_1[:]).then_inc(rows_ready, 1)
            nc.scalar.activation(row_first[:], key_of_i[:], ACT.Identity, bias=minus_edge[:]).then_inc(rows_ready, 1)
            for t in range(NT):
                act.wait_ge(adj_loaded[t], 16)
                nc.scalar.activation(adj16[:, t, :], adj_sb[:, t, :], ACT.Identity, accum_out=adj_sum[:, t:t + 1]).then_inc(adj16_made, 1)

            def direct_targets(first, end):
                for g in range(first, end):
                    t, s = divmod(g, DIRECT)
                    act.wait_ge(direct_indexed, t + 1)
                    nc.scalar.activation(off_i[:, g, :], key_of_i[:], ACT.Abs, scale=-1.0, bias=lists[:, t, s:s + 1]).then_inc(off_i_made, 1)
                for g in range(first, end):
                    act.wait_ge(off_i_made, g + 1)
                    nc.scalar.activation(direct_hot[:, g, :], off_i[:, g, :], ACT.Relu, scale=-1.0, bias=ones[:, 0:1]).then_inc(direct_hot_act, 1)

            def high(t):
                gs = slice(t * DIRECT, (t + 1) * DIRECT)
                act.wait_ge(prod_made, t + 1)
                nc.scalar.copy(high_part[:, gs, :], prod[:, gs, :]).then_inc(high_made, 1)

            act.wait_ge(ones_ready, 3)
            direct_targets(0, 1)
            act.wait_ge(ones2_ready, 1)
            nc.scalar.copy(take_rows01[:], rows01[:]).then_inc(take_rows_rounded, 1)
            act.wait_ge(bias_loaded, 48)
            nc.scalar.copy(bias_high[:], bias2[:]).then_inc(bias_high_made, 1)
            direct_targets(1, 3)
            act.wait_ge(x_loaded, 16)
            nc.scalar.copy(x_rest[:, :, 0:H], x_sb[:]).then_inc(x_rest_ready, 1)
            act.wait_ge(mid_made, 1)
            act.wait_ge(rank_consts, 3 + 2 * NT)
            for t, (a, b) in enumerate(WINDOWS):
                nc.scalar.activation(off_sq[:, t, 0:(b - a) * P], rank_odd[:, a * P:b * P], ACT.Square, scale=0.5,
                                     bias=minus_mid[:, t:t + 1]).then_inc(off_sq_made, 1)
            direct_targets(3, 4)
            high(0)
            direct_targets(4, 5)
            high(1)
            nc.scalar.activation(scratch[:], adj_sb[:].rearrange("p t i -> p (t i)"), ACT.Square, bias=half[:],
                                 accum_out=adj_off[:]).then_inc(adj_off_made, 1)
            direct_targets(5, ACT_TARGETS)
            high(2)
            high(3)
            act.wait_ge(guard_ready, 1)
            broken = act.value_load(bad_n[0:1, 0:1], min_val=0, max_val=P)
            act.wait_ge(agg_summed, 1)
            with act.If(broken == 0):
                for t in range(NT):
                    nc.scalar.copy(aggT[:, t * P:(t + 1) * P], agg_ps[:, t * P:(t + 1) * P]).then_inc(aggT_ready, 1)
            with act.Else():
                with act.Fori(0, LOADS // BUFFERS) as step:
                    for b in range(BUFFERS):
                        act.wait_ge(rows_summed[b], step + 1)
                        nc.scalar.copy(aggT[:, bass.ds((step * BUFFERS + b) * ROWS_PER_LOAD, ROWS_PER_LOAD)],
                                       rest_ps[:, b, 0:ROWS_PER_LOAD]).then_inc(rows_free[b], 1)
                for b in range(BUFFERS):
                    act.wait_ge(rows_free[b], LOADS // BUFFERS + 1)
                nc.scalar.copy(warm[:, 1:2], half[:]).then_inc(aggT_ready, NT)

            def gates(t):
                act.wait_ge(gates_summed, t + 1)
                nc.scalar.activation(rz[:, t, :], gru_ps[:, t, 0:2 * H], ACT.Sigmoid).then_inc(rz_made, 1)

            def new(t):
                act.wait_ge(pre_n_made, t + 1)
                nc.scalar.activation(n_gate[:, t, :], pre_n[:, t, :], ACT.Tanh).then_inc(n_made, 1)

            gates(0)
            for t in range(1, NT):
                gates(t)
                new(t - 1)
            new(NT - 1)
            nc.scalar.activation(warm[:, 0:1], eps[:], ACT.Sqrt).then_inc(warm_ready, 1)
            act.wait_ge(mv_made, NT)
            nc.scalar.activation(std[:], mv[:, :, 1], ACT.Sqrt, bias=eps[:]).then_inc(std_made, 1)
            act.wait_ge(shift_made, 1)
            for t in range(HALF, NT):
                nc.scalar.activation(out_sb[:, t, :], y[:, t, :], ACT.Identity, scale=rstd[:, t:t + 1],
                                     bias=shift[:, t:t + 1]).then_inc(out_made_act, 1)
            act.wait_ge(out_made_act, NT - HALF)
            act.dma_start(out_rows[:, HALF:NT, :], out_sb[:, HALF:NT, :]).then_inc(stored, 16)

        @block.tensor
        def _(pe):
            one16 = nc.const_aps.tensor(1.0, (P, 1), BF16)

            def keys(t):
                pe.wait_ge(adj16_made, t + 1)
                for row, bank in ((row_first, first_ps[t]), (row_last, last_ps[t])):
                    if bank is not None:
                        nc.tensor.matmul(bank, edge_diag[:], adj16[:, t, :], start=True, stop=False)
                        nc.tensor.matmul(bank, take_row0[:], row[:], start=False, stop=True).then_inc(keys_summed, 1)

            def gh(t):
                if t >= 1:
                    pe.wait_ge(first_made, t + 1)
                lhs = xT_sb[:, t * P:(t + 1) * P]
                nc.tensor.matmul(gru_ps[:, t, 0:2 * H], lhs, whh_sb[:, 0:2 * H], start=True, stop=False, skip_group_check=True)
                nc.tensor.matmul(gru_ps[:, t, G3:G3 + H], lhs, whh_sb[:, 2 * H:G3], start=False, stop=False, skip_group_check=True)

            def biases(t):
                for part in (bias_high, bias_low):
                    nc.tensor.matmul(gru_ps[:, t, :], take_rows01[:], part[:], start=False, stop=False, skip_group_check=True)

            for _ in range(WARM_UP):
                nc.tensor.matmul(gru_ps[:, 0, :], one16.to_broadcast([P, P]), one16.to_broadcast([P, N]), start=True, stop=True)
            pe.wait_ge(rows_ready, 2)
            pe.wait_ge(edge_diag_ready, 2)
            for t in range(NT):
                keys(t)
            pe.wait_ge(xT_loaded, 16)
            pe.wait_ge(w_loaded, 16)
            for t in range(NT):
                gh(t)
            pe.wait_ge(before_ready, 1)
            pe.wait_ge(rest_rounded, 1)
            nc.tensor.matmul(base_ps, before[:], rest_n16[:], start=True, stop=False, skip_group_check=True)
            for k in range(1, NT):
                mm = nc.tensor.matmul(base_ps[:, k:NT], ones16[:], rest_n16[:, 0:NT - k], start=False, stop=(k == NT - 1), skip_group_check=True)
            mm.then_inc(bases_summed, 1)
            pe.wait_ge(take_rows_rounded, 1)
            pe.wait_ge(bias_high_made, 1)
            pe.wait_ge(bias_low_made, 1)
            for t in range(NT):
                biases(t)

            pe.wait_ge(x_rest_ready, 4)
            for b, qs in enumerate(groups):
                for q in qs:
                    tiles = [t for t in range(NT) if WINDOWS[t][0] <= q < WINDOWS[t][1]]
                    pe.wait_ge(rank_hot_made, tiles[-1] + 1)
                    for t in tiles:
                        o = (q - WINDOWS[t][0]) * P
                        mm = nc.tensor.matmul(chunk_ps(q, 0, XR), rank_hot[:, t, o:o + P], x_rest[:, t, :],
                                              start=(t == tiles[0]), stop=(t == tiles[-1]))
                mm.then_inc(group_compacted, 1)

            for t in range(NT):
                if t == NT - 1:
                    pe.wait_ge(rest_indexed, BANKS)
                    pe.wait_ge(bad_made, 4)
                    nc.tensor.matmul(bad_ps, ones[:, 0:1], bad[:], start=False, stop=True, skip_group_check=True).then_inc(bad_counted, 1)
                pe.wait_ge(low_made, t + 1)
                pe.wait_ge(high_made, t + 1)
                for g in range(t * DIRECT, (t + 1) * DIRECT):
                    if g < ACT_TARGETS:
                        pe.wait_ge(direct_hot_act, g + 1)
                    else:
                        pe.wait_ge(direct_hot_dve, g + 1 - ACT_TARGETS)
                    nc.tensor.matmul(agg_ps[:], high_part[:, g, :], direct_hot[:, g, :], start=(g == 0), stop=False)
                    nc.tensor.matmul(agg_ps[:], low_part[:, g, :], direct_hot[:, g, :], start=False, stop=False)
            for q in range(CHUNKS):
                pe.wait_ge(rest_hot_made, q + 1)
                pe.wait_ge(prod_made, NT + q + 1)
                mm = nc.tensor.matmul(agg_ps[:], prod[:, NT * DIRECT + q, :], rest_hot[:, q, :],
                                      start=False, stop=(q == CHUNKS - 1))
            mm.then_inc(agg_summed, 1)

            pe.wait_ge(guard_ready, 1)
            broken = pe.value_load(bad_n[0:1, 0:1], min_val=0, max_val=P)
            with pe.If(broken != 0):
                pe.wait_ge(adj_f_made, 1)
                with pe.Fori(0, LOADS // BUFFERS) as step:
                    for b in range(BUFFERS):
                        pe.wait_ge(weighted[b], step + 1)
                        pe.wait_ge(rows_free[b], step + 1)
                        for r in range(ROWS_PER_LOAD):
                            for t in range(NT):
                                i = (step * BUFFERS + b) * ROWS_PER_LOAD + r
                                mm = nc.tensor.matmul(rest_ps[:, b, r:r + 1], table[:, b, r, t * H:(t + 1) * H],
                                                      adj_f[:, t, bass.ds(i, 1)], start=(t == 0), stop=(t == NT - 1))
                        mm.then_inc(rows_summed[b], 1)
                        nc.tensor.matmul(rest_ps[0:1, BUFFERS, 0:1], ones[:, 0:1], ones[:, 0:1], start=True, stop=True).then_inc(table_free[b], 1)
            pe.wait_ge(wih_loaded, 16)
            for t in range(NT):
                pe.wait_ge(aggT_ready, t + 1)
                nc.tensor.matmul(gru_ps[:, t, 0:G3], aggT[:, t * P:(t + 1) * P], wih_sb[:], start=False, stop=True,
                                 skip_group_check=True).then_inc(gates_summed, 1)

        @block.vector
        def _(dve):
            for value, at in ((-0.5, half), (EPS, eps), (-EDGE, minus_edge), (EDGE + N + 1, edge_n_1)):
                nc.vector.memset(at[:], value).then_inc(scalars_ready, 1)
            nc.vector.memset(edge[:], 0.0).then_inc(edge_zeroed, 1)

            def first(t):
                if t == 0:
                    dve.wait_ge(adj_loaded[0], 16)
                    nc.vector.tensor_tensor(keys0[:], adj_sb[:, 0, :], key_of_i[:], ALU.mult).then_inc(keys0_made, 1)
                    dve.wait_ge(keys0_made, 1)
                    nc.vector.max(lists[:, 0, 0:TOP], keys0[:]).then_inc(first_made, 1)
                else:
                    dve.wait_ge(keys_summed, 2 * t)
                    nc.vector.max(lists[:, t, 0:TOP], first_ps[t]).then_inc(first_made, 1)

            def last_ones(t):
                dve.wait_ge(keys_summed, 2 * t + 1)
                nc.vector.max(last[:, t, :], last_ps[t]).then_inc(last_made, 1)

            def index(t):
                dve.wait_ge(first_made, t + 1)
                nc.vector.tensor_scalar(idx_direct[:, t, :], lists[:, t, 0:DIRECT], float(-N), flat_of_j[:, t:t + 1],
                                        ALU.mult, ALU.add).then_inc(direct_indexed, 1)

            dve.wait_ge(key_of_i_ready, 1)
            first(0)
            dve.wait_ge(index_consts, 1)
            index(0)
            for t in range(1, NT):
                first(t)
                last_ones(t - 1)
                index(t)
            last_ones(NT - 1)
            dve.wait_ge(last_made, NT)
            nc.vector.tensor_scalar(last_key[:], last[:], -1.0, 2 * EDGE + N + 1, ALU.mult, ALU.add).then_inc(last_key_made, 1)
            dve.wait_ge(last_key_made, 1)
            nc.vector.tensor_tensor(is_new[:], last_key[:], lists[:, :, TOP - 1:TOP].to_broadcast([P, NT, TOP]),
                                    ALU.is_lt).then_inc(is_new_made, 1)
            dve.wait_ge(is_new_made, 1)
            nc.vector.tensor_tensor(lists[:, :, TOP:SLOTS], last_key[:], is_new[:], ALU.mult).then_inc(lists_made, 1)
            dve.wait_ge(lists_made, 1)
            nc.vector.tensor_scalar(filled[:], lists[:], EDGE, None, ALU.is_gt).then_inc(filled_made, 1)
            nc.vector.tensor_copy(x_rest[:, :, COL_LIST:COL_LIST + REST], lists[:, :, DIRECT:SLOTS]).then_inc(x_rest_ready, 1)
            dve.wait_ge(filled_made, 1)
            nc.vector.tensor_reduce(rest_n[:], filled[:, :, DIRECT:SLOTS], AX.X, ALU.add).then_inc(rest_counted, 1)
            dve.wait_ge(rest_counted, 1)
            nc.vector.tensor_copy(rest_n16[:], rest_n[:]).then_inc(rest_rounded, 1)
            nc.vector.tensor_reduce(found[:], filled[:], AX.X, ALU.add).then_inc(found_counted, 1)
            dve.wait_ge(rest_counted, 1)
            nc.vector.scalar_tensor_tensor(out=half_sq[:], in0=rest_n[:], scalar=0.25, in1=rest_n[:],
                                           op0=ALU.mult, op1=ALU.mult).then_inc(half_sq_made, 1)
            dve.wait_ge(bias_high_made, 1)
            nc.vector.tensor_tensor(bias_low[:], bias2[:], bias_high[:], ALU.subtract).then_inc(bias_low_made, 1)
            dve.wait_ge(bases_summed, 1)
            nc.vector.scalar_tensor_tensor(out=minus_mid[:], in0=rest_n[:], scalar=-0.5, in1=base_ps,
                                           op0=ALU.mult, op1=ALU.subtract).then_inc(mid_made, 1)
            nc.vector.tensor_copy(x_rest[:, :, COL_BASE], base_ps).then_inc(x_rest_ready, 1)
            dve.wait_ge(j_ready, 1)
            nc.vector.tensor_copy(x_rest[:, :, COL_J], j_of[:]).then_inc(x_rest_ready, 1)
            nc.vector.tensor_copy(base[:], base_ps).then_inc(base_made, 1)
            dve.wait_ge(base_made, 1)
            nc.vector.tensor_tensor(rest_end[:], base[:], rest_n[:], ALU.add).then_inc(rest_end_made, 1)

            def rank(t):
                w = (WINDOWS[t][1] - WINDOWS[t][0]) * P
                dve.wait_ge(off_sq_made, t + 1)
                nc.vector.tensor_scalar(rank_hot[:, t, 0:w], off_sq[:, t, 0:w], half_sq[:, t:t + 1], None,
                                        ALU.is_lt).then_inc(rank_hot_made, 1)

            def product(t):
                gs = slice(t * DIRECT, (t + 1) * DIRECT)
                for g in range(t * DIRECT, (t + 1) * DIRECT):
                    dve.wait_ge(gathered[g], 16)
                nc.vector.tensor_tensor(prod[:, gs, :], edge[:, gs, :], x_sb[:, t:t + 1, :].to_broadcast([P, DIRECT, H]),
                                        ALU.mult).then_inc(prod_made, 1)

            def low_of(t):
                gs = slice(t * DIRECT, (t + 1) * DIRECT)
                dve.wait_ge(high_made, t + 1)
                nc.vector.tensor_tensor(low_part[:, gs, :], prod[:, gs, :], high_part[:, gs, :], ALU.subtract).then_inc(low_made, 1)

            def rest_index(b):
                qs = slice(groups[b][0], groups[b][-1] + 1)
                dve.wait_ge(group_compacted, b + 1)
                nc.vector.tensor_tensor(slot_of[:, qs], rank_of[:, qs],
                                        group_ps(b, COL_BASE, COL_BASE + 1).rearrange("p q c -> p (q c)"), ALU.subtract).then_inc(slot_made, 1)
                nc.vector.tensor_scalar(flat_of_c[:, qs], group_ps(b, COL_J, COL_J + 1).rearrange("p q c -> p (q c)"),
                                        INVALID + EDGE * N, None, ALU.add).then_inc(slot_made, 1)
                dve.wait_ge(slot_made, 2 * b + 2)
                for q in groups[b]:
                    nc.vector.scalar_tensor_tensor(out=slot_key[:, q, :], in0=slot_iota[:], scalar=slot_of[:, q:q + 1],
                                                   in1=chunk_ps(q, COL_LIST, COL_LIST + REST), op0=ALU.is_equal, op1=ALU.mult,
                                                   accum_out=rest_key[:, q:q + 1]).then_inc(slot_key_made, 1)
                dve.wait_ge(slot_key_made, groups[b][-1] + 1)
                nc.vector.scalar_tensor_tensor(out=idx_rest[:, qs], in0=rest_key[:, qs], scalar=float(-N), in1=flat_of_c[:, qs],
                                               op0=ALU.mult, op1=ALU.add).then_inc(rest_indexed, 1)

            def direct_target_dve(first, end):
                for g in range(first, end):
                    t, s = divmod(g, DIRECT)
                    nc.vector.tensor_scalar(direct_hot[:, g, :], key_of_i[:], lists[:, t, s:s + 1], None, ALU.is_equal).then_inc(direct_hot_dve, 1)

            def rest_target(q):
                nc.vector.tensor_scalar(rest_hot[:, q, :], key_of_i[:], rest_key[:, q:q + 1], None, ALU.is_equal).then_inc(rest_hot_made, 1)

            rank(0)
            rank(1)
            rank(2)
            rank(3)
            product(0)
            rest_index(0)
            low_of(0)
            rest_index(1)
            rest_index(2)
            product(1)
            direct_target_dve(ACT_TARGETS, 9)
            low_of(1)
            dve.wait_ge(found_counted, 1)
            dve.wait_ge(adj16_made, NT)
            dve.wait_ge(rest_end_made, 1)
            nc.vector.tensor_tensor(bad[:, 0:NT], base[:], low[:], ALU.is_lt).then_inc(bad_made, 1)
            nc.vector.tensor_tensor(bad[:, NT:2 * NT], rest_end[:], high[:], ALU.is_gt).then_inc(bad_made, 1)
            nc.vector.tensor_tensor(bad[:, 2 * NT:3 * NT], adj_sum[:], found[:], ALU.not_equal).then_inc(bad_made, 1)
            product(2)
            direct_target_dve(9, NT * DIRECT)
            low_of(2)
            rest_target(0)
            rest_target(1)
            dve.wait_ge(adj_off_made, 1)
            nc.vector.tensor_scalar(bad[:, 3 * NT:BAD], adj_off[:], N * NT / 4, None, ALU.not_equal).then_inc(bad_made, 1)
            product(3)
            rest_target(2)
            low_of(3)
            rest_target(3)
            for q in range(CHUNKS):
                if q + 4 < CHUNKS:
                    rest_target(q + 4)
                g = NT * DIRECT + q
                dve.wait_ge(gathered[g], 16)
                nc.vector.tensor_tensor(prod[:, g, :], edge[:, g, :], chunk_ps(q, 0, H), ALU.mult).then_inc(prod_made, 1)
                if q == 1:
                    dve.wait_ge(bad_counted, 1)
                    nc.vector.tensor_reduce(bad_n[:], bad_ps, AX.X, ALU.max).then_inc(guard_ready, 1)

            dve.wait_ge(guard_ready, 1)
            broken = dve.value_load(bad_n[0:1, 0:1], min_val=0, max_val=P)
            with dve.If(broken != 0):
                nc.vector.tensor_copy(adj_f[:], adj_sb[:]).then_inc(adj_f_made, 1)
                for b in range(BUFFERS):
                    nc.vector.memset(credit[:, 2 * b:2 * b + 1], 0.0).then_inc(table_free[b], 1)
                    nc.vector.memset(credit[:, 2 * b + 1:2 * b + 2], 0.0).then_inc(rows_free[b], 1)
                with dve.Fori(0, LOADS // BUFFERS) as step:
                    for b in range(BUFFERS):
                        dve.wait_ge(table_loaded[b], (step + 1) * (16 * ROWS_PER_LOAD))
                        nc.vector.tensor_tensor(table[:, b], table[:, b],
                                                x_sb[:].rearrange("p t h -> p (t h)").unsqueeze(1).to_broadcast([P, ROWS_PER_LOAD, NT * H]),
                                                ALU.mult).then_inc(weighted[b], 1)

            def reset_n(t):
                dve.wait_ge(rz_made, t + 1)
                nc.vector.tensor_tensor(rh[:, t, :], rz[:, t, 0:H], gru_ps[:, t, G3:G3 + H], ALU.mult).then_inc(rh_made, 1)

            def pre(t):
                dve.wait_ge(rh_made, t + 1)
                nc.vector.tensor_tensor(pre_n[:, t, :], rh[:, t, :], gru_ps[:, t, 2 * H:G3], ALU.add).then_inc(pre_n_made, 1)

            def n_of(t):
                dve.wait_ge(n_made, t + 1)
                nc.vector.scalar_tensor_tensor(out=n_part[:, t, :], in0=rz[:, t, H:2 * H], scalar=-1.0, in1=n_gate[:, t, :],
                                               op0=ALU.add, op1=ALU.mult).then_inc(n_part_made, 1)

            def total(t):
                dve.wait_ge(n_part_made, t + 1)
                dve.wait_ge(x_part_made, t + 1)
                nc.vector.tensor_tensor(y[:, t, :], x_part[:, t, :], n_part[:, t, :], ALU.subtract).then_inc(y_made, 1)

            def moments(t):
                dve.wait_ge(y_made, t + 1)
                nc.vector.bn_stats(stats[:, t, :], y[:, t, :]).then_inc(stats_made, 1)

            def aggregate(t):
                dve.wait_ge(stats_made, t + 1)
                nc.vector.bn_aggr(mv[:, t, :], stats[:, t, :]).then_inc(mv_made, 1)

            for t in range(NT + 1):
                if t < NT:
                    reset_n(t)
                if t >= 2:
                    moments(t - 2)
                if t < NT:
                    pre(t)
                if t >= 2:
                    aggregate(t - 2)
                if t >= 1:
                    n_of(t - 1)
                    total(t - 1)
            moments(NT - 1)
            aggregate(NT - 1)
            dve.wait_ge(std_made, 1)
            nc.vector.reciprocal(rstd[:], std[:]).then_inc(rstd_made, 1)
            dve.wait_ge(rstd_made, 1)
            nc.vector.scalar_tensor_tensor(out=shift[:], in0=mv[:, :, 0], scalar=-1.0, in1=rstd[:],
                                           op0=ALU.mult, op1=ALU.mult).then_inc(shift_made, 1)
            for t in range(HALF):
                nc.vector.tensor_scalar(out_sb[:, t, :], y[:, t, :], mv[:, t, 0:1], rstd[:, t:t + 1],
                                        ALU.subtract, ALU.mult).then_inc(out_made, 1)


def kernel(x, adj, L0_gnn_edge_table, L0_gnn_w_ih, L0_gnn_w_hh, L0_gnn_b_ih, L0_gnn_b_hh):
    import numpy as np
    import concourse.bacc as bacc
    from concourse.bass_utils import run_bass_kernel_spmd

    x, adj, w_ih, w_hh = (np.asarray(a) for a in (x, adj, L0_gnn_w_ih, L0_gnn_w_hh))
    arrays = {
        "x": np.ascontiguousarray(x),
        "x_t": np.ascontiguousarray(x.T),
        "adj_t": np.ascontiguousarray(adj.T),
        "edge_table": np.ascontiguousarray(L0_gnn_edge_table),
        "w_ih_t": np.ascontiguousarray(w_ih.T),
        "w_hh_t": np.ascontiguousarray(w_hh.T),
        "b_ih": np.ascontiguousarray(L0_gnn_b_ih),
        "b_hh": np.ascontiguousarray(L0_gnn_b_hh),
    }
    nc = bacc.Bacc("TRN2", target_bir_lowering=False, num_devices=1)
    args = [nc.dram_tensor(name, a.shape, mybir.dt.from_np(a.dtype), kind="ExternalInput").ap()
            for name, a in arrays.items()]
    out = nc.dram_tensor("out", x.shape, F32, kind="ExternalOutput").ap()
    gnn_gru_norm(nc, *args, out)
    r = run_bass_kernel_spmd(nc, [arrays], core_ids=[0])
    return r.results[0]["out"]
```

```python
from contextlib import ExitStack

import concourse.bass as bass
from concourse import mybir

F32 = mybir.dt.float32
F32R = mybir.dt.float32r
F16 = mybir.dt.float16
BF16 = mybir.dt.bfloat16
I32 = mybir.dt.int32
ALU = mybir.AluOpType
ACT = mybir.ActivationFunctionType
AX = mybir.AxisListType

P = 128
TOP = 8
SLOTS = 2 * TOP
EDGE = 1024.0
DIRECT = 3
REST = SLOTS - DIRECT
WINDOWS = ((0, 2), (0, 4), (1, 5), (3, 7))
CHUNKS = WINDOWS[-1][1]
REST_STEPS = ((0, 2), (2, 3), (3, 4), (4, 5), (5, 6), (6, 7))
CHUNKS_PER_BANK = 3
BANK = 512
ROWS_PER_LOAD = 4
BUFFERS = 2
WARM_UP = 7
ACT_TARGETS = 7
ACT_REST = 2
POOL_SUMS = 2
EPS = 1e-5


def gnn_gru_norm(nc, x, x_t, adj_t, edge_table, w_ih_t, w_hh_t, b_ih, b_hh, out):
    N, H = x.shape
    NT = N // P
    G3 = 3 * H
    FLAT = (int(EDGE) + N) * N
    GATHERS = NT * DIRECT + CHUNKS
    COL_BASE, COL_J, COLS = REST, REST + 1, REST + 2
    BANKS = -(-CHUNKS // CHUNKS_PER_BANK)
    groups = [range(b * CHUNKS_PER_BANK, min((b + 1) * CHUNKS_PER_BANK, CHUNKS)) for b in range(BANKS)]
    BAD = 4 * NT
    LOADS = N // ROWS_PER_LOAD

    with ExitStack() as ctx:
        def sb(name, shape, dt=F32):
            return ctx.enter_context(nc.sbuf_tensor(name, shape, dt))

        def psum(name, shape):
            return ctx.enter_context(nc.psum_tensor(name, shape, F32))

        def sem(name):
            return ctx.enter_context(nc.semaphore(name))

        adj_sb = sb("adj_sb", [P, NT, N], I32)
        x_sb = sb("x_sb", [P, NT, H])
        xT_sb = sb("xT_sb", [P, N])
        wih_sb = sb("wih_sb", [P, G3])
        whh_sb = sb("whh_sb", [P, G3])
        bias2 = sb("bias2", [P, BANK])
        key_of_i = sb("key_of_i", [P, N])
        row_first = sb("row_first", [P, N], F16)
        row_last = sb("row_last", [P, N], F16)
        ones16 = sb("ones16", [P, P], F16)
        take_row0 = sb("take_row0", [P, P], F16)
        take_rows01 = sb("take_rows01", [P, P])
        edge_diag = sb("edge_diag", [P, P], BF16)
        minus_edge = sb("minus_edge", [P, 1])
        edge_n_1 = sb("edge_n_1", [P, 1])
        slot_iota = sb("slot_iota", [P, REST])
        flat_of_j = sb("flat_of_j", [P, CHUNKS])
        before = sb("before", [P, P], F16)
        ones = sb("ones", [P, P])
        low = sb("low", [P, NT])
        high = sb("high", [P, NT])
        window_mid = sb("window_mid", [P, NT])
        adj16 = sb("adj16", [P, NT, N], BF16)
        keys0 = sb("keys0", [P, N])
        lists = sb("lists", [P, NT, SLOTS])
        last = sb("last", [P, NT, TOP])
        last_key = sb("last_key", [P, NT, TOP])
        is_new = sb("is_new", [P, NT, TOP])
        filled = sb("filled", [P, NT, SLOTS])
        idx_direct = sb("idx_direct", [P, NT, DIRECT], I32)
        rest_n = sb("rest_n", [P, NT])
        rest_n16 = sb("rest_n16", [P, NT], F16)
        rest_end = sb("rest_end", [P, NT])
        half_x = sb("half_x", [P, NT, H])
        half_list = sb("half_list", [P, NT, COLS], F16)
        base = sb("base", [P, NT])
        half_n = sb("half_n", [P, NT])
        mid = sb("mid", [P, NT])
        half_sq = sb("half_sq", [P, NT])
        off_sq = sb("off_sq", [P, NT, 4 * P])
        rank_hot = sb("rank_hot", [P, NT, 4 * P])
        rank_hot16 = rank_hot[:].bitcast(F16).rearrange("p t (r two) -> p t r two", two=2)[:, :, :, 1]
        slot_of = sb("slot_of", [P, CHUNKS])
        flat_of_c = sb("flat_of_c", [P, CHUNKS])
        slot_key = sb("slot_key", [P, CHUNKS, REST])
        rest_key = sb("rest_key", [P, CHUNKS])
        idx_rest = sb("idx_rest", [P, CHUNKS], I32)
        edge = sb("edge", [P, GATHERS, H])
        prod = sb("prod", [P, GATHERS, H])
        high_part = sb("high_part", [P, GATHERS, H], F32R)
        low_part = sb("low_part", [P, GATHERS, H], F32R)
        off_i = sb("off_i", [P, ACT_TARGETS + ACT_REST, N])
        direct_hot = sb("direct_hot", [P, NT * DIRECT, N], F32R)
        rest_hot = sb("rest_hot", [P, CHUNKS - 1, N], F32R)
        last_hot = sb("last_hot", [P, N])
        aggT = sb("aggT", [P, N])
        agg_upper = sb("agg_upper", [P, N // 2])
        adj_sum = sb("adj_sum", [P, NT])
        found = sb("found", [P, NT])
        bad = sb("bad", [P, BAD])
        bad_n = sb("bad_n", [1, 1], I32)
        rz = sb("rz", [P, NT, 2 * H])
        rh = sb("rh", [P, NT, H])
        pre_n = sb("pre_n", [P, NT, H])
        n_gate = sb("n_gate", [P, NT, H])
        z1 = sb("z1", [P, NT, H])
        x_part = sb("x_part", [P, NT, H])
        n_part = sb("n_part", [P, NT, H])
        y = sb("y", [P, NT, H])
        stats = sb("stats", [P, NT, 6])
        mv = sb("mv", [P, NT, 2])
        rstd = sb("rstd", [P, NT])
        centred = sb("centred", [P, NT // 2, H])
        out_sb = sb("out_sb", [P, NT, H])
        warm = sb("warm", [P, 3])
        credit = sb("credit", [P, 2 * BUFFERS])
        eps = sb("eps", [P, 1])
        std = sb("std", [P, NT])
        adj_f = sb("adj_f", [P, NT, N])
        table = sb("table", [P, BUFFERS, ROWS_PER_LOAD, NT * H])

        agg_ps = psum("agg_ps", [P, BANK])
        gru_ps = psum("gru_ps", [P, NT, BANK])
        rest_ps = psum("rest_ps", [P, BANKS, BANK])
        upper_ps = rest_ps[:, 0, 0:N // 2]
        base_ps = rest_ps[:, BANKS - 1, BANK - 32:BANK - 32 + NT]
        bad_ps = rest_ps[0:1, BANKS - 1, BANK - 16:BANK - 16 + BAD]
        first_ps = [None] + [gru_ps[:, t, :] for t in range(1, NT)]
        last_ps = [agg_ps[:]] + [rest_ps[:, t, :] for t in range(NT - 1)]
        list_at = len(groups[-1]) * P
        list_ps = rest_ps[:, BANKS - 1, list_at:list_at + CHUNKS * COLS].rearrange("p (q c) -> p q c", q=CHUNKS)
        assert list_at + CHUNKS * COLS <= BANK - 32
        assert all((b - a) * P <= N for a, b in WINDOWS)
        assert BANKS >= BUFFERS + 1

        def rest_target(q):
            return rest_hot[:, q, :] if q < CHUNKS - 1 else last_hot[:]

        def x_ps(q):
            o = (q % CHUNKS_PER_BANK) * P
            return rest_ps[:, q // CHUNKS_PER_BANK, o:o + P]

        adj_loaded = [sem(f"adj_loaded{t}") for t in range(NT)]
        x_loaded, xT_loaded, w_loaded = sem("x_loaded"), sem("xT_loaded"), sem("w_loaded")
        wih_loaded, bias_loaded, key_of_i_ready = sem("wih_loaded"), sem("bias_loaded"), sem("key_of_i_ready")
        index_consts, rank_consts, edge_diag_ready = sem("index_consts"), sem("rank_consts"), sem("edge_diag_ready")
        rows_ready, ones_ready, ones2_ready = sem("rows_ready"), sem("ones_ready"), sem("ones2_ready")
        before_ready, scalars_ready, warm_ready = sem("before_ready"), sem("scalars_ready"), sem("warm_ready")
        bias_zeroed, edge_zeroed, windows_ready = sem("bias_zeroed"), sem("edge_zeroed"), sem("windows_ready")
        rest_zeroed = sem("rest_zeroed")
        adj16_made, keys0_made, keys_summed = sem("adj16_made"), sem("keys0_made"), sem("keys_summed")
        first_made, last_made, last_key_made = sem("first_made"), sem("last_made"), sem("last_key_made")
        is_new_made, lists_made, filled_made = sem("is_new_made"), sem("lists_made"), sem("filled_made")
        direct_indexed = sem("direct_indexed")
        rest_counted, rest_rounded, found_counted = sem("rest_counted"), sem("rest_rounded"), sem("found_counted")
        bases_summed, base_made, half_n_made = sem("bases_summed"), sem("base_made"), sem("half_n_made")
        half_sq_made, mid_made, off_sq_made = sem("half_sq_made"), sem("mid_made"), sem("off_sq_made")
        rank_hot_made, half_x_made, half_list_made = sem("rank_hot_made"), sem("half_x_made"), sem("half_list_made")
        lists_compacted, group_compacted, slot_made = sem("lists_compacted"), sem("group_compacted"), sem("slot_made")
        slot_key_made, rest_indexed, rest_end_made = sem("slot_key_made"), sem("rest_indexed"), sem("rest_end_made")
        prod_made, high_made, low_made = sem("prod_made"), sem("high_made"), sem("low_made")
        off_i_made, direct_hot_act, direct_hot_dve = sem("off_i_made"), sem("direct_hot_act"), sem("direct_hot_dve")
        rest_hot_act, rest_hot_dve, agg_summed = sem("rest_hot_act"), sem("rest_hot_dve"), sem("agg_summed")
        upper_copied, upper_ready, aggT_ready = sem("upper_copied"), sem("upper_ready"), sem("aggT_ready")
        bad_made, bad_counted, guard_ready = sem("bad_made"), sem("bad_counted"), sem("guard_ready")
        gates_summed, rz_made, z1_made = sem("gates_summed"), sem("rz_made"), sem("z1_made")
        rh_made, pre_n_made, n_made = sem("rh_made"), sem("pre_n_made"), sem("n_made")
        n_part_made, x_part_made, last_x_part_made = sem("n_part_made"), sem("x_part_made"), sem("last_x_part_made")
        y_made, y_pool, stats_made = sem("y_made"), sem("y_pool"), sem("stats_made")
        mv_made, std_made, rstd_made = sem("mv_made"), sem("std_made"), sem("rstd_made")
        centred_made, out_made, out_made_act = sem("centred_made"), sem("out_made"), sem("out_made_act")
        stored = sem("stored")
        gathered = [sem(f"gathered{g}") for g in range(GATHERS)]
        adj_f_made = sem("adj_f_made")
        table_loaded = [sem(f"table_loaded{b}") for b in range(BUFFERS)]
        table_free = [sem(f"table_free{b}") for b in range(BUFFERS)]
        weighted = [sem(f"weighted{b}") for b in range(BUFFERS)]
        rows_summed = [sem(f"rows_summed{b}") for b in range(BUFFERS)]
        rows_free = [sem(f"rows_free{b}") for b in range(BUFFERS)]

        out_rows = out.rearrange("(t p) h -> p t h", p=P)
        table_rows = edge_table.rearrange("(l r t p) h -> l r p t h", r=ROWS_PER_LOAD, t=NT, p=P)

        block = ctx.enter_context(nc.Block())

        @block.sync
        def _(sp):
            for t in range(NT):
                sp.dma_start(adj_sb[:, t, :], adj_t[t * P:(t + 1) * P, :]).then_inc(adj_loaded[t], 16)
            sp.dma_start(xT_sb[:], x_t).then_inc(xT_loaded, 16)
            sp.dma_start(whh_sb[:], w_hh_t).then_inc(w_loaded, 16)
            sp.wait_ge(bias_zeroed, 1)
            sp.dma_start(bias2[0:1, 0:G3], b_ih.rearrange("(a g) -> a g", a=1)).then_inc(bias_loaded, 16)
            sp.dma_start(bias2[1:2, 0:2 * H], b_hh[0:2 * H].rearrange("(a g) -> a g", a=1)).then_inc(bias_loaded, 16)
            sp.dma_start(bias2[1:2, G3:G3 + H], b_hh[2 * H:G3].rearrange("(a g) -> a g", a=1)).then_inc(bias_loaded, 16)
            sp.dma_start(x_sb[:], x.rearrange("(t p) h -> p t h", p=P)).then_inc(x_loaded, 16)
            sp.dma_start(wih_sb[:], w_ih_t).then_inc(wih_loaded, 16)
            sp.wait_ge(guard_ready, 1)
            broken = sp.value_load(bad_n[0:1, 0:1], min_val=0, max_val=P)
            with sp.If(broken != 0):
                with sp.Fori(0, LOADS // BUFFERS) as step:
                    for b in range(BUFFERS):
                        sp.wait_ge(table_free[b], step + 1)
                        for r in range(ROWS_PER_LOAD):
                            src = table_rows[bass.ds(step * BUFFERS + b, 1), r, :, :, :].rearrange("l p t h -> (l p) t h")
                            sp.dma_start(table[:, b, r, :].rearrange("p (t h) -> p t h", t=NT), src).then_inc(table_loaded[b], 16)
            sp.wait_ge(out_made, NT // 2)
            sp.dma_start(out_rows[:, NT // 2:NT, :], out_sb[:, NT // 2:NT, :]).then_inc(stored, 16)
            sp.wait_ge(stored, 32)

        @block.gpsimd
        def _(pool):
            nc.gpsimd.iota(key_of_i[:], [[-1, N]], base=N + int(EDGE), channel_multiplier=0,
                           allow_small_or_imprecise_dtypes=True).then_inc(key_of_i_ready, 1)
            pool.wait_ge(ones_ready, 3)
            nc.gpsimd.affine_select(out=edge_diag[:], in_=edge_diag[:], compare_op=ALU.not_equal, fill=EDGE, base=0,
                                    pattern=[[1, P]], channel_multiplier=-1).then_inc(edge_diag_ready, 1)
            nc.gpsimd.affine_select(out=take_row0[:], in_=ones16[:], compare_op=ALU.is_gt, fill=0.0, base=1,
                                    pattern=[[0, P]], channel_multiplier=-1).then_inc(edge_diag_ready, 1)
            nc.gpsimd.iota(flat_of_j[:], [[P, CHUNKS]], base=FLAT, channel_multiplier=1,
                           allow_small_or_imprecise_dtypes=True).then_inc(index_consts, 1)
            nc.gpsimd.memset(bias2[:], 0.0).then_inc(bias_zeroed, 1)
            nc.gpsimd.affine_select(out=take_rows01[:], in_=ones[:], compare_op=ALU.is_gt, fill=0.0, base=2,
                                    pattern=[[0, P]], channel_multiplier=-1).then_inc(ones2_ready, 1)
            nc.gpsimd.affine_select(out=before[:], in_=ones16[:], compare_op=ALU.is_gt, fill=0.0, base=0,
                                    pattern=[[1, P]], channel_multiplier=-1).then_inc(before_ready, 1)
            nc.gpsimd.iota(slot_iota[:], [[1, REST]], base=0, channel_multiplier=0,
                           allow_small_or_imprecise_dtypes=True).then_inc(rank_consts, 1)
            for t in range(NT):
                nc.gpsimd.memset(window_mid[:, t:t + 1], -(EDGE + N + WINDOWS[t][0] * P + 0.5)).then_inc(rank_consts, 1)
            for t in range(NT):
                nc.gpsimd.memset(low[:, t:t + 1], float(WINDOWS[t][0] * P)).then_inc(windows_ready, 1)
                nc.gpsimd.memset(high[:, t:t + 1], float(WINDOWS[t][1] * P)).then_inc(windows_ready, 1)
            pool.wait_ge(edge_zeroed, 1)
            for t in range(NT):
                pool.wait_ge(direct_indexed, t + 1)
                for s in range(DIRECT):
                    g = t * DIRECT + s
                    nc.gpsimd.indirect_dma_start(
                        out=edge[:, g, :], out_offset=None, in_=edge_table,
                        in_offset=bass.IndirectOffsetOnAxis(ap=idx_direct[:, t, s:s + 1], axis=0),
                        bounds_check=N * N - 1, oob_is_err=False).then_inc(gathered[g], 16)
            pool.wait_ge(rest_indexed, 1)
            pool.wait_ge(rest_zeroed, 2)
            for q in range(CHUNKS):
                g = NT * DIRECT + q
                nc.gpsimd.indirect_dma_start(
                    out=edge[:, g, :], out_offset=None, in_=edge_table,
                    in_offset=bass.IndirectOffsetOnAxis(ap=idx_rest[:, q:q + 1], axis=0),
                    bounds_check=N * N - 1, oob_is_err=False).then_inc(gathered[g], 16)

            def x_part_of(t):
                pool.wait_ge(z1_made, t + 1)
                nc.gpsimd.tensor_tensor(x_part[:, t, :], z1[:, t, :], x_sb[:, t, :], ALU.mult).then_inc(x_part_made, 1)

            def total_pool(t):
                pool.wait_ge(x_part_made, t + 1)
                pool.wait_ge(n_part_made, t + 1)
                nc.gpsimd.tensor_tensor(y[:, t, :], x_part[:, t, :], n_part[:, t, :], ALU.subtract).then_inc(y_pool, 1)

            x_part_of(0)
            for t in range(POOL_SUMS):
                x_part_of(t + 1)
                total_pool(t)
            for t in range(POOL_SUMS + 1, NT - 1):
                x_part_of(t)
            for t in range(NT // 2):
                pool.wait_ge(mv_made, t + 1)
                pool.wait_ge(y_pool, t + 1)
                nc.gpsimd.tensor_tensor(centred[:, t, :], y[:, t, :], mv[:, t, 0:1].to_broadcast([P, H]), ALU.subtract).then_inc(centred_made, 1)

        @block.scalar
        def _(act):
            act.wait_ge(scalars_ready, 3)
            nc.scalar.activation(warm[:, 0:1], eps[:], ACT.Sigmoid).then_inc(warm_ready, 1)
            act.wait_ge(key_of_i_ready, 1)
            nc.scalar.activation(row_last[:], key_of_i[:], ACT.Identity, scale=-1.0, bias=edge_n_1[:]).then_inc(rows_ready, 1)
            nc.scalar.activation(row_first[:], key_of_i[:], ACT.Identity, bias=minus_edge[:]).then_inc(rows_ready, 1)
            for t in range(NT):
                act.wait_ge(adj_loaded[t], 16)
                nc.scalar.activation(adj16[:, t, :], adj_sb[:, t, :], ACT.Identity, accum_out=adj_sum[:, t:t + 1]).then_inc(adj16_made, 1)

            def direct_targets(first, end):
                for g in range(first, end):
                    t, s = divmod(g, DIRECT)
                    act.wait_ge(direct_indexed, t + 1)
                    nc.scalar.activation(off_i[:, g, :], key_of_i[:], ACT.Abs, scale=-1.0, bias=lists[:, t, s:s + 1]).then_inc(off_i_made, 1)
                for g in range(first, end):
                    act.wait_ge(off_i_made, g + 1)
                    nc.scalar.activation(direct_hot[:, g, :], off_i[:, g, :], ACT.Relu, scale=-1.0, bias=ones[:, 0:1]).then_inc(direct_hot_act, 1)

            def rest_target_act(q):
                k = ACT_TARGETS + CHUNKS - 1 - q
                act.wait_ge(rest_indexed, 1)
                nc.scalar.activation(off_i[:, k, :], key_of_i[:], ACT.Abs, scale=-1.0, bias=rest_key[:, q:q + 1]).then_inc(off_i_made, 1)
                act.wait_ge(off_i_made, k + 1)
                nc.scalar.activation(rest_target(q), off_i[:, k, :], ACT.Relu, scale=-1.0, bias=ones[:, 0:1]).then_inc(rest_hot_act, 1)

            def high(t):
                gs = slice(t * DIRECT, (t + 1) * DIRECT)
                act.wait_ge(prod_made, t + 1)
                nc.scalar.copy(high_part[:, gs, :], prod[:, gs, :]).then_inc(high_made, 1)

            act.wait_ge(ones_ready, 3)
            direct_targets(0, DIRECT)
            act.wait_ge(x_loaded, 16)
            nc.scalar.activation(half_x[:], x_sb[:], ACT.Identity, scale=0.5).then_inc(half_x_made, 1)
            a, b = NT * DIRECT, NT * DIRECT + CHUNKS // 2
            for first_g, end_g in ((a, b), (b, GATHERS)):
                n = (end_g - first_g) * H
                nc.scalar.activation(edge[:, first_g:end_g, :].rearrange("p g h -> p (g h)"), key_of_i[:, 0:n],
                                     ACT.Identity, scale=0.0).then_inc(rest_zeroed, 1)
            act.wait_ge(mid_made, 1)
            for t, (a, b) in enumerate(WINDOWS):
                nc.scalar.activation(off_sq[:, t, 0:(b - a) * P], key_of_i[:, 0:(b - a) * P], ACT.Square,
                                     bias=mid[:, t:t + 1]).then_inc(off_sq_made, 1)
            direct_targets(3, 4)
            high(0)
            direct_targets(4, 5)
            high(1)
            high(2)
            direct_targets(5, 7)
            high(3)
            rest_target_act(CHUNKS - 1)
            for k, (a, b) in enumerate(REST_STEPS[:-1]):
                act.wait_ge(prod_made, NT + k + 1)
                nc.scalar.copy(high_part[:, NT * DIRECT + a:NT * DIRECT + b, :],
                               prod[:, NT * DIRECT + a:NT * DIRECT + b, :]).then_inc(high_made, 1)
                if k == 0:
                    rest_target_act(CHUNKS - 2)
            act.wait_ge(guard_ready, 1)
            broken = act.value_load(bad_n[0:1, 0:1], min_val=0, max_val=P)
            act.wait_ge(agg_summed, 1)
            with act.If(broken == 0):
                for t in range(NT // 2):
                    nc.scalar.copy(aggT[:, t * P:(t + 1) * P], agg_ps[:, t * P:(t + 1) * P]).then_inc(aggT_ready, 1)
                nc.scalar.copy(agg_upper[:], agg_ps[:, N // 2:N]).then_inc(upper_copied, 1)
            with act.Else():
                with act.Fori(0, LOADS // BUFFERS) as step:
                    for b in range(BUFFERS):
                        act.wait_ge(rows_summed[b], step + 1)
                        nc.scalar.copy(aggT[:, bass.ds((step * BUFFERS + b) * ROWS_PER_LOAD, ROWS_PER_LOAD)],
                                       rest_ps[:, b, 0:ROWS_PER_LOAD]).then_inc(rows_free[b], 1)
                for b in range(BUFFERS):
                    act.wait_ge(rows_free[b], LOADS // BUFFERS + 1)
                nc.scalar.copy(warm[:, 1:2], eps[:]).then_inc(aggT_ready, NT // 2)
                nc.scalar.copy(warm[:, 2:3], eps[:]).then_inc(upper_ready, 1)

            def gates(t):
                act.wait_ge(gates_summed, t + 1)
                nc.scalar.activation(rz[:, t, :], gru_ps[:, t, 0:2 * H], ACT.Sigmoid).then_inc(rz_made, 1)

            def one_plus_z(t):
                act.wait_ge(rz_made, t + 1)
                nc.scalar.activation(z1[:, t, :], rz[:, t, H:2 * H], ACT.Identity, bias=ones[:, 0:1]).then_inc(z1_made, 1)

            def new(t):
                act.wait_ge(pre_n_made, t + 1)
                nc.scalar.activation(n_gate[:, t, :], pre_n[:, t, :], ACT.Tanh).then_inc(n_made, 1)

            gates(0)
            one_plus_z(0)
            gates(1)
            new(0)
            one_plus_z(1)
            gates(2)
            new(1)
            gates(3)
            one_plus_z(2)
            new(2)
            new(3)
            nc.scalar.activation(warm[:, 0:1], eps[:], ACT.Sqrt).then_inc(warm_ready, 1)
            for first, end in ((0, NT - 1), (NT - 1, NT)):
                act.wait_ge(mv_made, end)
                nc.scalar.activation(std[:, first:end], mv[:, first:end, 1], ACT.Sqrt, bias=eps[:]).then_inc(std_made, 1)
            for t in range(NT // 2):
                act.wait_ge(centred_made, t + 1)
                act.wait_ge(rstd_made, 1)
                nc.scalar.activation(out_sb[:, t, :], centred[:, t, :], ACT.Identity, scale=rstd[:, t:t + 1]).then_inc(out_made_act, 1)
            act.wait_ge(out_made_act, NT // 2)
            act.dma_start(out_rows[:, 0:NT // 2, :], out_sb[:, 0:NT // 2, :]).then_inc(stored, 16)

        @block.tensor
        def _(pe):
            one16 = nc.const_aps.tensor(1.0, (P, 1), BF16)

            def keys(t):
                pe.wait_ge(adj16_made, t + 1)
                for row, bank in ((row_first, first_ps[t]), (row_last, last_ps[t])):
                    if bank is not None:
                        nc.tensor.matmul(bank, edge_diag[:], adj16[:, t, :], start=True, stop=False)
                        nc.tensor.matmul(bank, take_row0[:], row[:], start=False, stop=True).then_inc(keys_summed, 1)

            def gh(t):
                if t >= 1:
                    pe.wait_ge(first_made, t + 1)
                lhs = xT_sb[:, t * P:(t + 1) * P]
                nc.tensor.matmul(gru_ps[:, t, 0:2 * H], lhs, whh_sb[:, 0:2 * H], start=True, stop=False, skip_group_check=True)
                nc.tensor.matmul(gru_ps[:, t, G3:G3 + H], lhs, whh_sb[:, 2 * H:G3], start=False, stop=False, skip_group_check=True)

            def biases(t):
                nc.tensor.matmul(gru_ps[:, t, :], take_rows01[:], bias2[:], start=False, stop=False, skip_group_check=True)

            for _ in range(WARM_UP):
                nc.tensor.matmul(gru_ps[:, 0, :], one16.to_broadcast([P, P]), one16.to_broadcast([P, N]), start=True, stop=True)
            pe.wait_ge(rows_ready, 2)
            pe.wait_ge(edge_diag_ready, 2)
            for t in range(NT):
                keys(t)
            pe.wait_ge(xT_loaded, 16)
            pe.wait_ge(w_loaded, 16)
            for t in range(NT):
                gh(t)
            pe.wait_ge(ones2_ready, 1)
            pe.wait_ge(bias_loaded, 48)
            biases(0)
            pe.wait_ge(before_ready, 1)
            pe.wait_ge(rest_rounded, 1)
            nc.tensor.matmul(base_ps, before[:], rest_n16[:], start=True, stop=False, skip_group_check=True)
            for k in range(1, NT):
                mm = nc.tensor.matmul(base_ps[:, k:NT], ones16[:], rest_n16[:, 0:NT - k], start=False, stop=(k == NT - 1), skip_group_check=True)
            mm.then_inc(bases_summed, 1)
            for t in range(1, NT):
                biases(t)

            pe.wait_ge(half_list_made, 3)
            tiles_of = [[t for t in range(NT) if WINDOWS[t][0] <= q < WINDOWS[t][1]] for q in range(CHUNKS)]
            for q, tiles in enumerate(tiles_of):
                pe.wait_ge(rank_hot_made, tiles[-1] + 1)
                for t in tiles:
                    o = (q - WINDOWS[t][0]) * P
                    mm = nc.tensor.matmul(list_ps[:, q, :], rank_hot16[:, t, o:o + P], half_list[:, t, :],
                                          start=(t == tiles[0]), stop=(t == tiles[-1]))
            mm.then_inc(lists_compacted, 1)
            pe.wait_ge(half_x_made, 1)
            for q, tiles in enumerate(tiles_of):
                if q == groups[-1][0]:
                    pe.wait_ge(rest_indexed, 1)
                for t in tiles:
                    o = (q - WINDOWS[t][0]) * P
                    mm = nc.tensor.matmul(x_ps(q), rank_hot[:, t, o:o + P], half_x[:, t, :],
                                          start=(t == tiles[0]), stop=(t == tiles[-1]))
                if q == groups[q // CHUNKS_PER_BANK][-1]:
                    mm.then_inc(group_compacted, 1)

            def add(g, target):
                nc.tensor.matmul(agg_ps[:], high_part[:, g, :], target, start=(g == 0), stop=False)
                nc.tensor.matmul(agg_ps[:], low_part[:, g, :], target, start=False, stop=False)

            for t in range(NT):
                pe.wait_ge(low_made, t + 1)
                for g in range(t * DIRECT, (t + 1) * DIRECT):
                    if g < ACT_TARGETS:
                        pe.wait_ge(direct_hot_act, g + 1)
                    else:
                        pe.wait_ge(direct_hot_dve, g + 1 - ACT_TARGETS)
                    add(g, direct_hot[:, g, :])
            for k, (a, b) in enumerate(REST_STEPS[:-2]):
                if k == 1:
                    pe.wait_ge(bad_made, 4)
                    nc.tensor.matmul(bad_ps, ones[:, 0:1], bad[:], start=False, stop=True, skip_group_check=True).then_inc(bad_counted, 1)
                pe.wait_ge(rest_hot_dve, b)
                pe.wait_ge(low_made, NT + k + 1)
                for q in range(a, b):
                    add(NT * DIRECT + q, rest_hot[:, q, :])
            pe.wait_ge(rest_hot_act, ACT_REST)
            pe.wait_ge(low_made, NT + len(REST_STEPS) - 1)
            for columns, sums, start in ((slice(0, N // 2), agg_ps[:, 0:N // 2], False), (slice(N // 2, N), upper_ps, True)):
                target = rest_hot[:, CHUNKS - 2, columns]
                nc.tensor.matmul(sums, high_part[:, GATHERS - 2, :], target, start=start, stop=False)
                nc.tensor.matmul(sums, low_part[:, GATHERS - 2, :], target, start=False, stop=False)
                pe.wait_ge(prod_made, NT + len(REST_STEPS))
                nc.tensor.matmul(sums, prod[:, GATHERS - 1, :], last_hot[:, columns], start=False, stop=True).then_inc(agg_summed, 1)

            pe.wait_ge(guard_ready, 1)
            broken = pe.value_load(bad_n[0:1, 0:1], min_val=0, max_val=P)
            with pe.If(broken != 0):
                pe.wait_ge(adj_f_made, 1)
                with pe.Fori(0, LOADS // BUFFERS) as step:
                    for b in range(BUFFERS):
                        pe.wait_ge(weighted[b], step + 1)
                        pe.wait_ge(rows_free[b], step + 1)
                        for r in range(ROWS_PER_LOAD):
                            for t in range(NT):
                                i = (step * BUFFERS + b) * ROWS_PER_LOAD + r
                                mm = nc.tensor.matmul(rest_ps[:, b, r:r + 1], table[:, b, r, t * H:(t + 1) * H],
                                                      adj_f[:, t, bass.ds(i, 1)], start=(t == 0), stop=(t == NT - 1))
                        mm.then_inc(rows_summed[b], 1)
                        nc.tensor.matmul(rest_ps[0:1, BUFFERS, 0:1], ones[:, 0:1], ones[:, 0:1], start=True, stop=True).then_inc(table_free[b], 1)
            pe.wait_ge(wih_loaded, 16)
            for t in range(NT):
                if t < NT // 2:
                    pe.wait_ge(aggT_ready, t + 1)
                else:
                    pe.wait_ge(upper_ready, 1)
                nc.tensor.matmul(gru_ps[:, t, 0:G3], aggT[:, t * P:(t + 1) * P], wih_sb[:], start=False, stop=True,
                                 skip_group_check=True).then_inc(gates_summed, 1)

        @block.vector
        def _(dve):
            for value, at in ((EPS, eps), (-EDGE, minus_edge), (EDGE + N + 1, edge_n_1)):
                nc.vector.memset(at[:], value).then_inc(scalars_ready, 1)
            for value, at in ((0.0, edge_diag), (1.0, ones16), (1.0, ones)):
                nc.vector.memset(at[:], value).then_inc(ones_ready, 1)
            nc.vector.memset(edge[:, 0:NT * DIRECT, :], 0.0).then_inc(edge_zeroed, 1)

            def first(t):
                if t == 0:
                    dve.wait_ge(adj_loaded[0], 16)
                    nc.vector.tensor_tensor(keys0[:], adj_sb[:, 0, :], key_of_i[:], ALU.mult).then_inc(keys0_made, 1)
                    dve.wait_ge(keys0_made, 1)
                    nc.vector.max(lists[:, 0, 0:TOP], keys0[:]).then_inc(first_made, 1)
                else:
                    dve.wait_ge(keys_summed, 2 * t)
                    nc.vector.max(lists[:, t, 0:TOP], first_ps[t]).then_inc(first_made, 1)

            def last_ones(t):
                dve.wait_ge(keys_summed, 2 * t + 1)
                nc.vector.max(last[:, t, :], last_ps[t]).then_inc(last_made, 1)

            def index(t):
                dve.wait_ge(first_made, t + 1)
                nc.vector.tensor_scalar(idx_direct[:, t, :], lists[:, t, 0:DIRECT], float(-N), flat_of_j[:, t:t + 1],
                                        ALU.mult, ALU.add).then_inc(direct_indexed, 1)

            dve.wait_ge(key_of_i_ready, 1)
            first(0)
            dve.wait_ge(index_consts, 1)
            index(0)
            for t in range(1, NT):
                first(t)
                last_ones(t - 1)
                index(t)
            last_ones(NT - 1)
            dve.wait_ge(last_made, NT)
            nc.vector.tensor_scalar(last_key[:], last[:], -1.0, 2 * EDGE + N + 1, ALU.mult, ALU.add).then_inc(last_key_made, 1)
            dve.wait_ge(last_key_made, 1)
            nc.vector.tensor_tensor(is_new[:], last_key[:], lists[:, :, TOP - 1:TOP].to_broadcast([P, NT, TOP]),
                                    ALU.is_lt).then_inc(is_new_made, 1)
            dve.wait_ge(is_new_made, 1)
            nc.vector.tensor_tensor(lists[:, :, TOP:SLOTS], last_key[:], is_new[:], ALU.mult).then_inc(lists_made, 1)
            dve.wait_ge(lists_made, 1)
            nc.vector.tensor_scalar(filled[:], lists[:], EDGE, None, ALU.is_gt).then_inc(filled_made, 1)
            nc.vector.tensor_scalar(half_list[:, :, 0:REST], lists[:, :, DIRECT:SLOTS], 0.5, None, ALU.mult).then_inc(half_list_made, 1)
            dve.wait_ge(filled_made, 1)
            nc.vector.tensor_reduce(rest_n[:], filled[:, :, DIRECT:SLOTS], AX.X, ALU.add).then_inc(rest_counted, 1)
            dve.wait_ge(rest_counted, 1)
            nc.vector.tensor_copy(rest_n16[:], rest_n[:]).then_inc(rest_rounded, 1)
            nc.vector.tensor_reduce(found[:], filled[:], AX.X, ALU.add).then_inc(found_counted, 1)
            dve.wait_ge(rest_counted, 1)
            nc.vector.scalar_tensor_tensor(out=half_sq[:], in0=rest_n[:], scalar=0.25, in1=rest_n[:],
                                           op0=ALU.mult, op1=ALU.mult).then_inc(half_sq_made, 1)
            dve.wait_ge(rank_consts, 1 + NT)
            nc.vector.scalar_tensor_tensor(out=half_n[:], in0=rest_n[:], scalar=0.5, in1=window_mid[:],
                                           op0=ALU.mult, op1=ALU.add).then_inc(half_n_made, 1)
            nc.vector.tensor_scalar(half_list[:, :, COL_J], flat_of_j[:, 0:NT], float(-FLAT), 0.5, ALU.add, ALU.mult).then_inc(half_list_made, 1)
            dve.wait_ge(bases_summed, 1)
            dve.wait_ge(half_n_made, 1)
            nc.vector.tensor_tensor(mid[:], base_ps, half_n[:], ALU.add).then_inc(mid_made, 1)
            nc.vector.tensor_scalar(half_list[:, :, COL_BASE], base_ps, 0.5, None, ALU.mult).then_inc(half_list_made, 1)
            nc.vector.tensor_copy(base[:], base_ps).then_inc(base_made, 1)
            dve.wait_ge(base_made, 1)
            nc.vector.tensor_tensor(rest_end[:], base[:], rest_n[:], ALU.add).then_inc(rest_end_made, 1)

            def rank(t):
                w = (WINDOWS[t][1] - WINDOWS[t][0]) * P
                dve.wait_ge(off_sq_made, t + 1)
                nc.vector.tensor_scalar(rank_hot[:, t, 0:w], off_sq[:, t, 0:w], half_sq[:, t:t + 1], 2.0,
                                        ALU.is_lt, ALU.mult).then_inc(rank_hot_made, 1)

            def product(t):
                gs = slice(t * DIRECT, (t + 1) * DIRECT)
                for g in range(t * DIRECT, (t + 1) * DIRECT):
                    dve.wait_ge(gathered[g], 16)
                nc.vector.tensor_tensor(prod[:, gs, :], edge[:, gs, :], x_sb[:, t:t + 1, :].to_broadcast([P, DIRECT, H]),
                                        ALU.mult).then_inc(prod_made, 1)

            def low_of(t):
                gs = slice(t * DIRECT, (t + 1) * DIRECT)
                dve.wait_ge(high_made, t + 1)
                nc.vector.tensor_tensor(low_part[:, gs, :], prod[:, gs, :], high_part[:, gs, :], ALU.subtract).then_inc(low_made, 1)

            def rest_index():
                dve.wait_ge(lists_compacted, 1)
                nc.vector.scalar_tensor_tensor(out=slot_of[:], in0=flat_of_j[:], scalar=float(-FLAT), in1=list_ps[:, :, COL_BASE],
                                               op0=ALU.add, op1=ALU.subtract).then_inc(slot_made, 1)
                nc.vector.tensor_scalar(flat_of_c[:], list_ps[:, :, COL_J], FLAT, None, ALU.add).then_inc(slot_made, 1)
                dve.wait_ge(slot_made, 2)
                for q in range(CHUNKS):
                    nc.vector.scalar_tensor_tensor(out=slot_key[:, q, :], in0=slot_iota[:], scalar=slot_of[:, q:q + 1],
                                                   in1=list_ps[:, q, 0:REST], op0=ALU.is_equal, op1=ALU.mult,
                                                   accum_out=rest_key[:, q:q + 1]).then_inc(slot_key_made, 1)
                dve.wait_ge(slot_key_made, CHUNKS)
                nc.vector.scalar_tensor_tensor(out=idx_rest[:], in0=rest_key[:], scalar=float(-N), in1=flat_of_c[:],
                                               op0=ALU.mult, op1=ALU.add).then_inc(rest_indexed, 1)

            def direct_target_dve(first, end):
                for g in range(first, end):
                    t, s = divmod(g, DIRECT)
                    nc.vector.tensor_scalar(direct_hot[:, g, :], key_of_i[:], lists[:, t, s:s + 1], None, ALU.is_equal).then_inc(direct_hot_dve, 1)

            def rest_target_dve(q):
                nc.vector.tensor_scalar(rest_target(q), key_of_i[:], rest_key[:, q:q + 1], None, ALU.is_equal).then_inc(rest_hot_dve, 1)

            rank(0)
            rank(1)
            rank(2)
            rank(3)
            def rest_product(k):
                a, b = REST_STEPS[k]
                g = NT * DIRECT
                dve.wait_ge(group_compacted, a // CHUNKS_PER_BANK + 1)
                for q in range(a, b):
                    dve.wait_ge(gathered[g + q], 16)
                o = (a % CHUNKS_PER_BANK) * P
                nc.vector.tensor_tensor(prod[:, g + a:g + b, :].rearrange("p q h -> p (q h)"),
                                        edge[:, g + a:g + b, :].rearrange("p q h -> p (q h)"),
                                        rest_ps[:, a // CHUNKS_PER_BANK, o:o + (b - a) * P], ALU.mult).then_inc(prod_made, 1)

            def rest_low(k):
                gs = slice(NT * DIRECT + REST_STEPS[k][0], NT * DIRECT + REST_STEPS[k][1])
                dve.wait_ge(high_made, NT + k + 1)
                nc.vector.tensor_tensor(low_part[:, gs, :], prod[:, gs, :], high_part[:, gs, :], ALU.subtract).then_inc(low_made, 1)

            product(0)
            rest_index()
            product(1)
            product(2)
            low_of(0)
            direct_target_dve(ACT_TARGETS, 8)
            low_of(1)
            direct_target_dve(8, 9)
            low_of(2)
            direct_target_dve(9, 10)
            product(3)
            direct_target_dve(10, NT * DIRECT)
            low_of(3)
            rest_target_dve(0)
            rest_product(0)
            rest_target_dve(1)
            dve.wait_ge(windows_ready, 2 * NT)
            nc.vector.tensor_tensor(bad[:, 0:NT], base[:], low[:], ALU.is_lt).then_inc(bad_made, 1)
            dve.wait_ge(rest_end_made, 1)
            nc.vector.tensor_tensor(bad[:, NT:2 * NT], rest_end[:], high[:], ALU.is_gt).then_inc(bad_made, 1)
            dve.wait_ge(found_counted, 1)
            dve.wait_ge(adj16_made, NT)
            nc.vector.tensor_tensor(bad[:, 2 * NT:3 * NT], adj_sum[:], found[:], ALU.not_equal).then_inc(bad_made, 1)
            nc.vector.tensor_scalar(bad[:, 3 * NT:BAD], lists[:, :, 0], EDGE + N, None, ALU.is_gt).then_inc(bad_made, 1)
            rest_low(0)
            rest_target_dve(2)
            rest_product(1)
            rest_target_dve(3)
            rest_low(1)
            rest_product(2)
            rest_target_dve(4)
            rest_product(3)
            rest_low(2)
            dve.wait_ge(bad_counted, 1)
            nc.vector.tensor_reduce(bad_n[:], bad_ps, AX.X, ALU.max).then_inc(guard_ready, 1)
            rest_product(4)
            rest_low(3)
            rest_low(4)
            rest_product(5)

            dve.wait_ge(guard_ready, 1)
            broken = dve.value_load(bad_n[0:1, 0:1], min_val=0, max_val=P)
            with dve.If(broken == 0):
                dve.wait_ge(agg_summed, 2)
                dve.wait_ge(upper_copied, 1)
                nc.vector.tensor_tensor(aggT[:, N // 2:N], agg_upper[:], upper_ps, ALU.add).then_inc(upper_ready, 1)
            with dve.Else():
                nc.vector.tensor_copy(adj_f[:], adj_sb[:]).then_inc(adj_f_made, 1)
                for b in range(BUFFERS):
                    nc.vector.memset(credit[:, 2 * b:2 * b + 1], 0.0).then_inc(table_free[b], 1)
                    nc.vector.memset(credit[:, 2 * b + 1:2 * b + 2], 0.0).then_inc(rows_free[b], 1)
                with dve.Fori(0, LOADS // BUFFERS) as step:
                    for b in range(BUFFERS):
                        dve.wait_ge(table_loaded[b], (step + 1) * (16 * ROWS_PER_LOAD))
                        nc.vector.tensor_tensor(table[:, b], table[:, b],
                                                x_sb[:].rearrange("p t h -> p (t h)").unsqueeze(1).to_broadcast([P, ROWS_PER_LOAD, NT * H]),
                                                ALU.mult).then_inc(weighted[b], 1)

            def reset_n(t):
                dve.wait_ge(rz_made, t + 1)
                nc.vector.tensor_tensor(rh[:, t, :], rz[:, t, 0:H], gru_ps[:, t, G3:G3 + H], ALU.mult).then_inc(rh_made, 1)

            def pre(t):
                dve.wait_ge(rh_made, t + 1)
                nc.vector.tensor_tensor(pre_n[:, t, :], rh[:, t, :], gru_ps[:, t, 2 * H:G3], ALU.add).then_inc(pre_n_made, 1)

            def n_of(t):
                dve.wait_ge(n_made, t + 1)
                nc.vector.scalar_tensor_tensor(out=n_part[:, t, :], in0=rz[:, t, H:2 * H], scalar=-1.0, in1=n_gate[:, t, :],
                                               op0=ALU.add, op1=ALU.mult).then_inc(n_part_made, 1)

            def last_x_part():
                dve.wait_ge(rz_made, NT)
                nc.vector.scalar_tensor_tensor(out=x_part[:, NT - 1, :], in0=rz[:, NT - 1, H:2 * H], scalar=1.0,
                                               in1=x_sb[:, NT - 1, :], op0=ALU.add, op1=ALU.mult).then_inc(last_x_part_made, 1)

            def total(t):
                dve.wait_ge(n_part_made, t + 1)
                if t < NT - 1:
                    dve.wait_ge(x_part_made, t + 1)
                else:
                    dve.wait_ge(last_x_part_made, 1)
                nc.vector.tensor_tensor(y[:, t, :], x_part[:, t, :], n_part[:, t, :], ALU.subtract).then_inc(y_made, 1)

            def moments(t):
                if t < POOL_SUMS:
                    dve.wait_ge(y_pool, t + 1)
                else:
                    dve.wait_ge(y_made, t + 1 - POOL_SUMS)
                nc.vector.bn_stats(stats[:, t, :], y[:, t, :]).then_inc(stats_made, 1)

            def aggregate(t):
                dve.wait_ge(stats_made, t + 1)
                nc.vector.bn_aggr(mv[:, t, :], stats[:, t, :]).then_inc(mv_made, 1)

            reset_n(0)
            pre(0)
            reset_n(1)
            pre(1)
            n_of(0)
            reset_n(2)
            n_of(1)
            pre(2)
            reset_n(3)
            last_x_part()
            pre(3)
            moments(0)
            n_of(2)
            aggregate(0)
            moments(1)
            total(2)
            aggregate(1)
            n_of(3)
            moments(2)
            total(3)
            aggregate(2)
            moments(3)

            def inverse(k, first, end):
                dve.wait_ge(std_made, k + 1)
                nc.vector.reciprocal(rstd[:, first:end], std[:, first:end]).then_inc(rstd_made, 1)

            def normalise(t, k):
                dve.wait_ge(rstd_made, k + 1)
                nc.vector.tensor_scalar(out_sb[:, t, :], y[:, t, :], mv[:, t, 0:1], rstd[:, t:t + 1],
                                        ALU.subtract, ALU.mult).then_inc(out_made, 1)

            aggregate(3)
            inverse(0, 0, NT - 1)
            normalise(2, 0)
            inverse(1, NT - 1, NT)
            normalise(3, 1)


def kernel(x, adj, L0_gnn_edge_table, L0_gnn_w_ih, L0_gnn_w_hh, L0_gnn_b_ih, L0_gnn_b_hh):
    import numpy as np
    import concourse.bacc as bacc
    from concourse.bass_utils import run_bass_kernel_spmd

    x, adj, w_ih, w_hh = (np.asarray(a) for a in (x, adj, L0_gnn_w_ih, L0_gnn_w_hh))
    arrays = {
        "x": np.ascontiguousarray(x),
        "x_t": np.ascontiguousarray(x.T),
        "adj_t": np.ascontiguousarray(adj.T),
        "edge_table": np.ascontiguousarray(L0_gnn_edge_table),
        "w_ih_t": np.ascontiguousarray(w_ih.T),
        "w_hh_t": np.ascontiguousarray(w_hh.T),
        "b_ih": np.ascontiguousarray(L0_gnn_b_ih),
        "b_hh": np.ascontiguousarray(L0_gnn_b_hh),
    }
    nc = bacc.Bacc("TRN2", target_bir_lowering=False, num_devices=1)
    args = [nc.dram_tensor(name, a.shape, mybir.dt.from_np(a.dtype), kind="ExternalInput").ap()
            for name, a in arrays.items()]
    out = nc.dram_tensor("out", x.shape, F32, kind="ExternalOutput").ap()
    gnn_gru_norm(nc, *args, out)
    r = run_bass_kernel_spmd(nc, [arrays], core_ids=[0])
    return r.results[0]["out"]
```
